# Optimizing a Trainium2 kernel written in Bass

```python
import numpy as np
import jax
import jax.numpy as jnp

def _softmax(x, axis=-1):
    return jax.nn.softmax(x, axis=axis)

def _gelu(x):
    return jax.nn.gelu(x, approximate=True)

def _silu(x):
    return jax.nn.silu(x)

def _sigmoid(x):
    return jax.nn.sigmoid(x)

def _layernorm(x, axis=-1, eps=1e-05):
    m = jnp.mean(x, axis=axis, keepdims=True)
    v = jnp.var(x, axis=axis, keepdims=True)
    return (x - m) / jnp.sqrt(v + eps)

def _scatter_add(tgt, idx, src, axis=0):
    return tgt.at[idx].add(src)

def _segment_sum(src, seg, n):
    return jax.ops.segment_sum(src, seg, n)
kernel_name = 'mk_cond_resid_d1_seqx_r2_324d77'

def setup_inputs(seed: int=0):
    np.random.seed(seed)
    _w = jnp.asarray

    def _rec_inputs():
        import jax
        import jax.numpy as jnp
        _rk = jax.random.key(seed)
        x = 7.22e-05 + 1 * jax.random.normal(jax.random.fold_in(_rk, 1), (16, 512, 1024), jnp.float32)
        _lenS = 512 - jax.random.randint(jax.random.fold_in(_rk, 7), (16,), 0, max(1, 512 // 4) + 1, jnp.int32)
        _lenS2 = 512 - jax.random.randint(jax.random.fold_in(_rk, 8), (16,), 0, max(1, 512 // 4) + 1, jnp.int32)
        cond_2048 = jax.random.bernoulli(jax.random.fold_in(_rk, 11), 0.5063, (16, 1024)).astype(jnp.float32)
        return (x, cond_2048)
    x, cond_2048 = _rec_inputs()

    def _L0_cond_setup():
        import jax, jax.numpy as jnp
        import numpy as np
        NH = 8
        NEG = -1e+30
        key = jax.random.key(seed)
        k1, k2, k3, k4 = jax.random.split(key, 4)
        B, D, T = (4, 512, 1024)
        x = jax.random.normal(k1, (B, D, T), dtype=jnp.float32)
        mask = jax.random.randint(k2, (B, T), 0, 2).astype(jnp.float32)
        lim = float(np.sqrt(6.0 / (D + D)))
        Wq = jax.random.uniform(k3, (D, D), dtype=jnp.float32, minval=-lim, maxval=lim)
        Wo = jax.random.uniform(k4, (D, D), dtype=jnp.float32, minval=-lim, maxval=lim)
        return {'x': x, 'mask': mask, 'Wq': Wq, 'Wo': Wo}
    _L0_cond_all = _L0_cond_setup()
    _L0_cond_in = {k: v for k, v in _L0_cond_all.items() if k in ('Wq', 'Wo')}
    del _L0_cond_all
    return {'x': x, 'cond_2048': cond_2048, 'L0_cond_Wq': _L0_cond_in['Wq'], 'L0_cond_Wo': _L0_cond_in['Wo']}

def reference(x, cond_2048, L0_cond_Wq, L0_cond_Wo):
    import jax
    import jax.numpy as jnp

    def _L0_cond_ref(x, mask, Wq, Wo):
        import jax, jax.numpy as jnp
        import numpy as np
        NH = 8
        NEG = -1e+30
        B, D, T = x.shape
        dk = D // NH
        scale = 1.0 / jnp.sqrt(jnp.asarray(dk, x.dtype))
        xt = jnp.transpose(x, (0, 2, 1))
        q = xt @ Wq.T
        qh = q.reshape(B, T, NH, dk).transpose(0, 2, 1, 3)
        scores = scale * jnp.einsum('bhqd,bhkd->bhqk', qh, qh)
        cmask = mask[:, None, None, :]
        rmask = mask[:, None, :, None]
        logits = (scores * cmask + (1.0 - cmask) * NEG) * rmask
        attn = jax.nn.softmax(logits, axis=-1)
        ctx = jnp.einsum('bhqk,bhkd->bhqd', attn, qh)
        ctx = ctx.transpose(0, 2, 1, 3).reshape(B, T, D)
        out = ctx @ Wo.T
        return jnp.transpose(out, (0, 2, 1))
    x = x + _L0_cond_ref(x, cond_2048, L0_cond_Wq, L0_cond_Wo)
    return x

_drawn_inputs = setup_inputs


def setup_inputs(seed=0):
    import zlib

    import numpy as np

    out = dict(_drawn_inputs(seed))
    spreads = {}
    factors = {}
    for name, (base, spread) in spreads.items():
        noise = np.random.default_rng([zlib.crc32(name.encode()), seed]).standard_normal(out[name].shape)
        drawn = base * np.exp(spread * noise) if base else spread * noise
        out[name] = jnp.asarray(drawn.astype(out[name].dtype))
    for name, factor in factors.items():
        out[name] = (out[name] * factor).astype(out[name].dtype)
    return out
```

```python
from contextlib import ExitStack

import concourse.bass as bass
from concourse import mybir

P = 128
F32 = mybir.dt.float32
F32R = mybir.dt.float32r
BF16 = mybir.dt.bfloat16
F16 = mybir.dt.float16
I32 = mybir.dt.int32
ALU = mybir.AluOpType
ACT = mybir.ActivationFunctionType
AX = mybir.AxisListType

HEADS = 8
DK = 64
PAIRS = HEADS // 2
NEG = -1e30
SLOTS = 4
OPA, OPB, OPY, OPX = range(4)


class Form:

    def __init__(self, name, NT, R, T, NP, NA):
        self.name, self.NT, self.R, self.T = name, NT, R, T
        self.C = NT * R
        self.H = self.C // 2
        self.NTALL = -(-T // R)
        self.RL = T - R * (self.NTALL - 1)
        self.NTAIL = self.NTALL - NT
        self.NP, self.NA = NP, NA

    def rows(self, k):
        return self.RL if k == self.NTALL - 1 else self.R


def misc_jobs(form, has_prev, has_next):
    NT = form.NT
    table = {(h, k): [] for h in range(HEADS) for k in range(NT)}
    outs = [(0, 3), (0, 4), (0, 4), (1, 0), (1, 1)] if NT == 5 else \
        [(0, 4), (0, 5), (0, 6), (0, 6), (0, 7), (0, 7), (1, 0), (1, 1)]
    xts = [(3, 3), (3, 3), (3, 4), (3, 4), (4, 0)] if NT == 5 else \
        [(3, 4), (3, 4), (3, 5), (3, 5), (3, 6), (3, 6), (3, 7), (3, 7)]
    for h in range(HEADS):
        if h < HEADS - 1 or has_next:
            table[h, 0].append(("mT", h + 1))
        if h % 2 == 0 and (h < 4 or has_next):
            table[h, 1].append(("proj", (h // 2 + 2, 0)))
            table[h, 3].append(("proj", (h // 2 + 2, 1)))
        if h % 2 == 1 and (h < 7 or has_next):
            table[h, 1] += [("V", ((h + 1) // 2, 0)), ("V", ((h + 1) // 2, 1))]
        if h > 0 or has_prev:
            table[h, 2].append(("L", h - 1))
    if has_prev:
        for k, at in enumerate(outs):
            table[at].append(("out", k))
    if has_next:
        for k, at in enumerate(xts):
            table[at].append(("xT", k))
        table[5, 0].append(("xbar", 0))
        table[5, 3].append(("w", 0))
    return table


def front_jobs(form):
    return ([("xT", k, -1) for k in range(form.NT)] + [("xbar", 0, -1), ("w", 0, -1)]
            + [("proj", (g, half), 0) for g in range(2) for half in range(2)]
            + [("V", (0, 0), 0), ("V", (0, 1), 0), ("mT", 0, 0)])


def tail_jobs(form):
    return [("L", -1, 0)] + [("out", k, 0) for k in range(form.NT)]


def with_banks(form):
    def give(jobs, start, two_back):
        out = []
        for i, (name, arg, back) in enumerate(jobs):
            out.append((name, arg, (start + i) % 2, two_back[-2]))
            two_back = [two_back[-1], (name, arg, back)]
        return out, two_back

    def give_table(table, start, two_back):
        steps = list(table)
        flat, two_back = give([(*job, 0) for at in steps for job in table[at]], start, two_back)
        flat = iter(flat)
        return {at: [next(flat) for _ in table[at]] for at in steps}, two_back

    def one_later(two_back):
        return [(name, arg, back - 1) for name, arg, back in two_back]

    def count(table):
        return sum(map(len, table.values()))

    tables = [misc_jobs(form, False, True), misc_jobs(form, True, True), misc_jobs(form, True, False)]
    assert count(tables[1]) % 2 == 0
    front, end = give(front_jobs(form), 0, [None, None])
    at = len(front)
    first, end = give_table(tables[0], at, end)
    at += count(tables[0])
    mid, same_end = give_table(tables[1], at, one_later(end))
    assert same_end == end
    last, end = give_table(tables[2], at, one_later(end))
    tail, _ = give(tail_jobs(form), at + count(tables[2]), one_later(end))
    return front, first, mid, last, tail


def at_least(eng, sem, value):
    if not isinstance(value, int) or value > 0:
        eng.wait_ge(sem, value)


def wait_alone(eng, sem, value, passed):
    if not isinstance(value, int) or value > 0:
        eng.wait_ge(sem, value)
        eng.sem_inc(passed, 1)


def attention_kernel(nc, x_rows, mask_t, wq, wqT, woT, out_rows, B, T, D):
    KD = D // P
    TT = T // P
    forms = [Form("small", 5, 116, T, 4, 2), Form("full", 8, 128, T, 2, 1)]
    SCALE = float(DK) ** -0.5

    with ExitStack() as ctx:
        def sb(name, shape, dt, stack=ctx):
            return stack.enter_context(nc.sbuf_tensor(name, shape, dt))

        def psum(name, shape, dt):
            return ctx.enter_context(nc.psum_tensor(name, shape, dt))

        def sem(name):
            return ctx.enter_context(nc.semaphore(name))

        ST = [psum(f"scores{i}", [P, 2, 512], F32) for i in range(2)]
        MX = psum("max_scores", [P, 512], F32)
        CT = psum("ctx_psum", [P, 512], F32)
        MB = [psum(f"misc{i}", [P, 512], F32) for i in range(2)]

        wqT_sb = sb("wqT_sb", [P, KD, D], F32)
        woT_sb = sb("woT_sb", [P, KD, D], F32)
        G = sb("G", [P, KD, D], F32)
        ident = sb("ident", [P, P], F32)
        identR = sb("identR", [P, P], F32R)
        ones64 = sb("ones64", [P, DK], F32)
        meanT = sb("meanT", [P, P], F32)
        n_all = sb("n_all", [P, B], F32)
        n_max = sb("n_max", [P, 1], F32)
        n_max_i = sb("n_max_i", [P, 1], I32)
        pos = sb("pos", [P, TT, B], F32)
        tokid = sb("tokid", [P, TT, B], F32)

        sems = {n: sem(n) for n in (
            "loaded mask_loaded consts_made iotas_made consts_cast mask_cast counted pos_step pos_done g_made g_kept "
            "place_step onehots_made perm_made idx_made jidx_made ops_cleared").split()}
        loaded, mask_loaded, consts_made, iotas_made, consts_cast, mask_cast, counted, pos_step, pos_done, g_made, \
            g_kept, place_step, onehots_made, perm_made, idx_made, jidx_made, ops_cleared = sems.values()
        s_ready, mx_ready, pv_done = sem("s_ready"), sem("mx_ready"), sem("pv_done")
        xT_ready, xbar_ready, w_ready = sem("xT_ready"), sem("xbar_ready"), sem("w_ready")
        proj_ready, v_ready, mT_ready = sem("proj_ready"), sem("v_ready"), sem("mT_ready")
        l_ready, out_ready = sem("l_ready"), sem("out_ready")
        exp_done, xT_kept, hi_done, v_kept = sem("exp_done"), sem("xT_kept"), sem("hi_done"), sem("v_kept")
        xbar_kept, w_kept, ct_kept = sem("xbar_kept"), sem("w_kept"), sem("ct_kept")
        mx_red, mcol_done, mrow_done, lo_done = sem("mx_red"), sem("mcol_done"), sem("mrow_done"), sem("lo_done")
        ctx_done, xv_done, xsum_step, mask_step = sem("ctx_done"), sem("xv_done"), sem("xsum_step"), sem("mask_step")
        out_step, out_done, rsum_done = sem("out_step"), sem("out_done"), sem("rsum_done")
        pacc_step, idx_copied, tail_added = sem("pacc_step"), sem("idx_copied"), sem("tail_added")
        sp_passed, pool_passed = sem("sp_passed"), sem("pool_passed")
        dup = [sem(f"dup{i}") for i in range(SLOTS)]
        mrow_put = [sem(f"mrow_put{i}") for i in range(2)]
        gathered, gathered_tail = sem("gathered"), sem("gathered_tail")
        scattered, scattered_tail = sem("scattered"), sem("scattered_tail")

        tensors = [{} for _ in forms]
        for f, t in zip(forms, tensors):
            def keep(name, shape, dt, stack=ctx, t=t, f=f):
                t[name] = sb(f"{f.name}_{name}", shape, dt, stack)

            keep("idx", [P, B, f.NTALL], I32)
            keep("jidx", [P, f.NTALL], F32)
            keep("idx_cur", [P, 2, f.NTALL], I32)
            keep("valid", [P, 2, f.NT], F32)
            keep("inv", [P, 2, f.NT], F32)
            keep("kbias", [P, 2, f.NT], F32)

        start = ExitStack()
        wq_sb = sb("wq_sb", [P, KD, D], F32, start)
        mask_f = sb("mask_f", [P, TT, B], F32, start)
        mask_b = sb("mask_b", [P, TT, B], BF16, start)
        tri = sb("tri", [P, P], BF16, start)
        ones_b = sb("ones_b", [P, P], BF16, start)
        cnt = sb("cnt", [P, TT, B], F32, start)
        behind = sb("behind", [P, TT, B], F32, start)
        tokid_i = sb("tokid_i", [P, TT, B], I32, start)
        start.close()

        for f, t in zip(forms, tensors):
            own = ExitStack()

            def keep(name, shape, dt, stack=own, t=t, f=f):
                t[name] = sb(f"{f.name}_{name}", shape, dt, stack)

            keep("xg", [P, 2, f.NTALL, D], F32)
            keep("xcT", [P, KD, f.C], F32)
            tables = ExitStack()
            t["jh"] = sb(f"{f.name}_jh", [P, TT, B], F32, tables)
            t["jl"] = sb(f"{f.name}_jl", [P, TT, B], F32, tables)
            t["tileno"] = sb(f"{f.name}_tileno", [P, f.NTALL], F32, tables)
            t["tileno_i"] = sb(f"{f.name}_tileno_i", [P, f.NTALL], I32, tables)
            t["rowno"] = sb(f"{f.name}_rowno", [P, f.R], F32, tables)
            t["rowno_i"] = sb(f"{f.name}_rowno_i", [P, f.R], I32, tables)
            t["jidx_i"] = sb(f"{f.name}_jidx_i", [P, f.NTALL], I32, tables)
            t["boff_i"] = sb(f"{f.name}_boff_i", [P, B, f.NTALL], I32, tables)
            t["boff"] = sb(f"{f.name}_boff", [P, B, f.NTALL], F32, tables)
            t["hot_tile_f"] = sb(f"{f.name}_hot_tile_f", [P, TT, B, f.NTALL], F32, tables)
            t["hot_tile"] = sb(f"{f.name}_hot_tile", [P, TT, B, f.NTALL], F16, tables)
            t["hot_row"] = sb(f"{f.name}_hot_row", [P, TT, B, f.R], F16, tables)
            tables.close()
            keep("ops", [P, SLOTS, 4, f.C], F32R)
            keep("H", [P, 2, f.C], F32R)
            keep("L", [P, 2, f.C], F32R)
            keep("V", [P, 2, f.NT, P], F32)
            keep("Pt", [P, f.NP, 2, f.H], F32)
            keep("Pacc", [P, f.NA, 2, f.H], F32)
            keep("ctxraw", [P, f.H], F32)
            keep("rsum", [P, f.H], F32)
            keep("ctxT", [P, KD, f.C], F32)
            keep("w", [P, 2, D], F32)
            keep("xbarT", [P, KD, P], F32)
            keep("xsum", [P, D], F32)
            keep("xv", [P, f.NA, D], F32)
            keep("mxp", [P, 2, f.NT, 2], F32)
            keep("mcol", [P, 2, f.NT], F32)
            keep("mrow", [f.NT, 2, f.R], F32R)
            own.close()

        block = ctx.enter_context(nc.Block())
        plans = [with_banks(f) for f in forms]

        def run_batches(eng, form, plan, batch, tail):
            front, first, mid, last, tail_plan = plan
            batch(0, 0, first, False, True)
            batch(1, 1, mid, True, True)
            with eng.Fori(2, B - 2, 2) as b:
                batch(b, 0, mid, True, True)
                batch(b + 1, 1, mid, True, True)
            batch(B - 2, 0, mid, True, True)
            batch(B - 1, 1, last, True, False)
            tail(tail_plan)

        def either_form(eng, body):
            eng.wait_ge(pos_done, 2)
            n = eng.value_load(n_max_i[0:1, 0:1], min_val=0, max_val=T)
            with eng.If(n <= forms[0].C):
                body(forms[0], tensors[0], plans[0])
            with eng.Else():
                body(forms[1], tensors[1], plans[1])

        @block.sync
        def _(sp):
            sp.dma_start(mask_f[:].rearrange("p t b -> p (t b)"), mask_t).then_inc(mask_loaded, 16)
            for dst, src in ((wq_sb, wq), (woT_sb, woT), (wqT_sb, wqT)):
                sp.dma_start(dst[:], src.rearrange("(k p) n -> p k n", p=P)).then_inc(loaded, 16)

            def body(f, t, plan):
                NT, R = f.NT, f.R

                def copy_operands(s, h):
                    slot, r0, stage = h % SLOTS, DK * (h % 2), (h // 2) % 2
                    hi = t["H"][r0:r0 + DK, stage, :]
                    lo = t["L"][r0:r0 + DK, stage, :]
                    wait_alone(sp, lo_done, s - h % 2 + 2, sp_passed)
                    wait_alone(sp, s_ready, NT * (s - SLOTS + 1), sp_passed)
                    for op, half, src in ((OPA, 0, hi), (OPA, 1, lo), (OPB, 0, hi), (OPB, 1, hi), (OPY, 0, hi),
                                          (OPX, 0, lo)):
                        sp.dma_start(t["ops"][DK * half:DK * half + DK, slot, op, :].bitcast(F32),
                                     src.bitcast(F32)).then_inc(dup[slot], 16)

                def put_max_row(s, h):
                    wait_alone(sp, mrow_done, s + 1, sp_passed)
                    sp.dma_start(t["ops"][DK:DK + 1, h % SLOTS, OPX, :].bitcast(F32).rearrange("o (k r) -> o k r", r=R),
                                 t["mrow"][:, h % 2, :].bitcast(F32)).then_inc(mrow_put[h % 2], 16)

                sp.wait_ge(ops_cleared, 1)
                copy_operands(0, 0)
                copy_operands(1, 1)
                copy_operands(2, 2)
                put_max_row(0, 0)

                def batch(b, par, table, has_prev, has_next):
                    for h in range(HEADS):
                        s = HEADS * b + h
                        if h < HEADS - 1 or has_next:
                            put_max_row(s + 1, h + 1)
                        if h < HEADS - 3 or has_next:
                            copy_operands(s + 3, h + 3)

                run_batches(sp, f, plan, batch, lambda tail: None)

            either_form(sp, body)

        @block.gpsimd
        def _(pool):
            nc.gpsimd.memset(ident[:], 0.0).then_inc(consts_made, 1)
            nc.gpsimd.memset(tri[:], 1.0).then_inc(consts_made, 1)
            nc.gpsimd.memset(ones_b[:], 1.0).then_inc(consts_made, 1)
            nc.gpsimd.memset(ones64[:], 1.0).then_inc(consts_made, 1)
            nc.gpsimd.memset(meanT[:], 1.0 / T).then_inc(consts_made, 1)
            pool.wait_ge(consts_made, 5)
            nc.gpsimd.affine_select(out=ident[:], in_=ident[:], compare_op=ALU.not_equal, fill=1.0, base=0,
                                    pattern=[[-1, P]], channel_multiplier=1).then_inc(consts_made, 1)
            nc.gpsimd.affine_select(out=tri[:], in_=tri[:], compare_op=ALU.is_ge, fill=0.0, base=0,
                                    pattern=[[1, P]], channel_multiplier=-1).then_inc(consts_made, 1)
            nc.gpsimd.iota(tokid_i[:], pattern=[[P, TT], [0, B]], base=0, channel_multiplier=1).then_inc(iotas_made, 1)

            def body(f, t, plan):
                NT, R, NTALL, NTAIL = f.NT, f.R, f.NTALL, f.NTAIL
                nc.gpsimd.iota(t["tileno_i"][:], pattern=[[1, NTALL]], base=0, channel_multiplier=0).then_inc(iotas_made, 1)
                nc.gpsimd.iota(t["rowno_i"][:], pattern=[[1, R]], base=0, channel_multiplier=0).then_inc(iotas_made, 1)
                nc.gpsimd.iota(t["jidx_i"][:], pattern=[[R, NTALL]], base=0, channel_multiplier=1).then_inc(iotas_made, 1)
                nc.gpsimd.iota(t["boff_i"][:], pattern=[[T, B], [0, NTALL]], base=0, channel_multiplier=0).then_inc(iotas_made, 1)
                pool.wait_ge(idx_made, 1)

                def gather(b, par):
                    at_least(pool, scattered, 16 * NT * (b - 1))
                    at_least(pool, scattered_tail, 16 * NTAIL * (b - 1))
                    nc.gpsimd.tensor_copy(t["idx_cur"][:R, par, :], t["idx"][:R, b, :]).then_inc(idx_copied, 1)
                    wait_alone(pool, idx_copied, b + 1, pool_passed)
                    for k in range(NTALL):
                        r = f.rows(k)
                        nc.gpsimd.indirect_dma_start(
                            out=t["xg"][:r, par, k, :], out_offset=None, in_=x_rows,
                            in_offset=bass.IndirectOffsetOnAxis(ap=t["idx_cur"][:r, par, k:k + 1], axis=0),
                        ).then_inc(gathered if k < NT else gathered_tail, 16)

                def scatter(par, k, done):
                    r = f.rows(k)
                    nc.gpsimd.indirect_dma_start(
                        out=out_rows, in_=t["xg"][:r, par, k, :], in_offset=None,
                        out_offset=bass.IndirectOffsetOnAxis(ap=t["idx_cur"][:r, par, k:k + 1], axis=0),
                    ).then_inc(done, 16)

                def finish_tail(b, par):
                    if NTAIL:
                        at_least(pool, w_kept, b + 1)
                        at_least(pool, xsum_step, (NTALL - 1) * (b + 1))
                        for i in range(NTAIL):
                            r, xk = f.rows(NT + i), t["xg"][:, par, NT + i, :]
                            nc.gpsimd.tensor_tensor(xk[:r], xk[:r], t["w"][:r, par, :], ALU.add).then_inc(tail_added, 1)
                        wait_alone(pool, tail_added, NTAIL * (b + 1), pool_passed)
                        for i in range(NTAIL):
                            scatter(par, NT + i, scattered_tail)

                def add_tile(s, h, k):
                    acc, p0 = t["Pacc"][:R, h % f.NA], (NT * h + k) % f.NP
                    if k == 1:
                        at_least(pool, l_ready, s - f.NA + 1)
                        other = t["Pt"][:R, (NT * h) % f.NP]
                    else:
                        pool.wait_ge(pacc_step, (NT - 1) * s + k - 1)
                        other = acc
                    pool.wait_ge(exp_done, NT * s + k + 1)
                    nc.gpsimd.tensor_tensor(acc, other, t["Pt"][:R, p0], ALU.add).then_inc(pacc_step, 1)

                gather(0, 0)
                finish_tail(0, 0)

                def batch(b, par, table, has_prev, has_next):
                    for h in range(HEADS):
                        s = HEADS * b + h
                        for k in range(1, NT):
                            add_tile(s, h, k)
                            if h == 1 and k == 3 and has_prev:
                                wait_alone(pool, out_done, NT * b, pool_passed)
                                for i in range(NT):
                                    scatter(1 - par, i, scattered)
                            if h == 2 and k == 1 and has_next:
                                gather(b + 1, 1 - par)
                            if h == 6 and k == 2 and has_next:
                                finish_tail(b + 1, 1 - par)

                def tail(jobs):
                    for i in range(NT):
                        pool.wait_ge(out_done, NT * (B - 1) + i + 1)
                        scatter((B - 1) % 2, i, scattered)
                    pool.wait_ge(scattered, 16 * NT * B)
                    at_least(pool, scattered_tail, 16 * NTAIL * B)

                run_batches(pool, f, plan, batch, tail)

            either_form(pool, body)

        @block.scalar
        def _(act):
            for k in range(KD):
                act.wait_ge(g_made, k + 1)
                nc.scalar.copy(G[:, k, :], MB[k % 2][:, 0:D]).then_inc(g_kept, 1)

            def body(f, t, plan):
                NT, R, C, H = f.NT, f.R, f.C, f.H

                def job(name, arg, bank, b, par):
                    if name == "xT":
                        act.wait_ge(xT_ready, NT * (b + 1) + arg + 1)
                        at_least(act, proj_ready, 2 * PAIRS * (b + 1))
                        nc.scalar.copy(t["xcT"][:, :, R * arg:R * arg + R],
                                       MB[bank][:, 0:KD * R].rearrange("p (c r) -> p c r", c=KD)).then_inc(xT_kept, 1)
                    elif name == "xbar":
                        act.wait_ge(xbar_ready, b + 2)
                        at_least(act, w_ready, b + 1)
                        nc.scalar.copy(t["xbarT"][:].rearrange("p k n -> p (k n)"), MB[bank][:, 0:KD * P]).then_inc(xbar_kept, 1)
                    elif name == "w":
                        act.wait_ge(w_ready, b + 2)
                        at_least(act, out_done, NT * b)
                        at_least(act, tail_added, f.NTAIL * b)
                        nc.scalar.copy(t["w"][:, 1 - par, :], MB[bank][:, 0:D]).then_inc(w_kept, 1)
                    elif name == "proj":
                        g, half = arg
                        p = PAIRS * b + g
                        act.wait_ge(proj_ready, 2 * p + half + 1)
                        at_least(act, dup[(2 * g) % SLOTS], 96 * (2 * b + g // 2))
                        at_least(act, dup[(2 * g + 1) % SLOTS], 96 * (2 * b + g // 2))
                        at_least(act, v_ready, 2 * p - 2)
                        nc.scalar.copy(t["H"][:, g % 2, half * H:half * H + H], MB[bank][:, 0:H]).then_inc(hi_done, 1)
                    elif name == "V":
                        g, part = arg
                        p = PAIRS * b + g
                        n = min(4, NT - 4 * part)
                        act.wait_ge(v_ready, 2 * p + part + 1)
                        at_least(act, pv_done, NT * (2 * p - 2))
                        nc.scalar.copy(t["V"][:R, g % 2, 4 * part:4 * part + n, :],
                                       MB[bank][:R, 0:n * P].rearrange("r (k c) -> r k c", k=n)).then_inc(v_kept, 1)

                def keep_ctx(s, h):
                    act.wait_ge(pv_done, NT * (s + 1))
                    at_least(act, ctx_done, s)
                    nc.scalar.copy(t["ctxraw"][:], CT[:, 0:H]).then_inc(ct_kept, 1)

                for name, arg, bank, before in plan[0]:
                    job(name, arg, bank, 0 if name in ("proj", "V") else -1, 1)

                def batch(b, par, table, has_prev, has_next):
                    for h in range(HEADS):
                        s = HEADS * b + h
                        for k in range(NT):
                            if k == 1 and (h > 0 or has_prev):
                                keep_ctx(s - 1, h - 1)
                            n = NT * s + k
                            act.wait_ge(s_ready, n + 1)
                            if h == 0 and k == 0:
                                act.wait_ge(mask_step, 3 * (b + 1))
                            at_least(act, pv_done, n - f.NP + 1)
                            ko, so = k - f.NP, s
                            while ko < 0:
                                ko, so = ko + NT, so - 1
                            at_least(act, pacc_step, (NT - 1) * so + max(ko, 1))
                            nc.scalar.activation(t["Pt"][:R, (NT * h + k) % f.NP], ST[(NT * h + k) % 2][:R, :, 0:H],
                                                 ACT.Exp, bias=t["kbias"][:R, par, k:k + 1],
                                                 scale=SCALE).then_inc(exp_done, 1)
                            for name, arg, bank, before in table[h, k]:
                                job(name, arg, bank, b, par)

                def tail(jobs):
                    keep_ctx(HEADS * B - 1, HEADS - 1)

                run_batches(act, f, plan, batch, tail)

            either_form(act, body)

        @block.vector
        def _(dve):
            dve.wait_ge(mask_loaded, 16)
            nc.vector.tensor_copy(mask_b[:], mask_f[:]).then_inc(mask_cast, 1)
            dve.wait_ge(iotas_made, 1)
            nc.vector.tensor_copy(tokid[:], tokid_i[:]).then_inc(pos_step, 1)
            dve.wait_ge(consts_made, 7)
            nc.vector.tensor_copy(identR[:], ident[:]).then_inc(consts_cast, 1)
            dve.wait_ge(counted, 1)
            nc.vector.tensor_copy(cnt[:].rearrange("p t b -> p (t b)"), ST[0][:, 0, 0:TT * B]).then_inc(pos_step, 1)
            nc.vector.tensor_copy(n_all[:], ST[0][:, 1, 0:B]).then_inc(pos_step, 1)
            dve.wait_ge(pos_step, 3)
            nc.vector.tensor_tensor(behind[:], tokid[:], cnt[:], ALU.subtract).then_inc(pos_step, 1)
            nc.vector.tensor_reduce(n_max[:], n_all[:], AX.X, ALU.max).then_inc(pos_step, 1)
            dve.wait_ge(pos_step, 5)
            nc.vector.tensor_tensor(behind[:], behind[:], n_all[:].unsqueeze(1).to_broadcast([P, TT, B]),
                                    ALU.add).then_inc(pos_step, 1)
            nc.vector.tensor_copy(n_max_i[:], n_max[:]).then_inc(pos_done, 1)
            dve.wait_ge(pos_step, 6)
            nc.vector.scalar_tensor_tensor(out=cnt[:], in0=cnt[:], scalar=-1.0, in1=behind[:], op0=ALU.add,
                                           op1=ALU.subtract).then_inc(pos_step, 1)
            dve.wait_ge(pos_step, 7)
            nc.vector.tensor_tensor(cnt[:], cnt[:], mask_f[:], ALU.mult).then_inc(pos_step, 1)
            dve.wait_ge(pos_step, 8)
            nc.vector.tensor_tensor(pos[:], cnt[:], behind[:], ALU.add).then_inc(pos_done, 1)

            def body(f, t, plan):
                NT, R, C, H, NTALL = f.NT, f.R, f.C, f.H, f.NTALL
                chain = 0

                dve.wait_ge(iotas_made, 5)
                nc.vector.tensor_copy(t["tileno"][:], t["tileno_i"][:]).then_inc(place_step, 1)
                nc.vector.tensor_copy(t["rowno"][:], t["rowno_i"][:]).then_inc(place_step, 1)
                nc.vector.tensor_copy(t["jidx"][:], t["jidx_i"][:]).then_inc(jidx_made, 1)
                nc.vector.tensor_copy(t["boff"][:], t["boff_i"][:]).then_inc(place_step, 1)
                nc.vector.tensor_scalar(t["jh"][:], pos[:], float(R), None, ALU.is_ge).then_inc(place_step, 1)
                chain = 4
                for i in range(2, NTALL):
                    dve.wait_ge(place_step, chain)
                    nc.vector.scalar_tensor_tensor(out=t["jh"][:], in0=pos[:], scalar=float(R * i), in1=t["jh"][:],
                                                   op0=ALU.is_ge, op1=ALU.add).then_inc(place_step, 1)
                    chain += 1
                dve.wait_ge(place_step, chain)
                nc.vector.scalar_tensor_tensor(out=t["jl"][:], in0=t["jh"][:], scalar=-float(R), in1=pos[:],
                                               op0=ALU.mult, op1=ALU.add).then_inc(place_step, 1)
                hot_shape = [P, TT * B, NTALL]
                flat = lambda a: a[:].rearrange("p t b -> p (t b)").unsqueeze(2).to_broadcast(hot_shape)
                hot_f = t["hot_tile_f"][:].rearrange("p t b i -> p (t b) i")
                nc.vector.tensor_tensor(hot_f, t["tileno"][:].unsqueeze(1).to_broadcast(hot_shape), flat(t["jh"]),
                                        ALU.is_equal).then_inc(place_step, 1)
                chain += 2
                dve.wait_ge(place_step, chain)
                nc.vector.tensor_tensor(t["hot_tile"][:].rearrange("p t b i -> p (t b) i"), hot_f, flat(tokid),
                                        ALU.mult).then_inc(onehots_made, 1)
                for tt in range(TT):
                    nc.vector.tensor_tensor(t["hot_row"][:, tt], t["rowno"][:].unsqueeze(1).to_broadcast([P, B, R]),
                                            t["jl"][:, tt, :].unsqueeze(2).to_broadcast([P, B, R]),
                                            ALU.is_equal).then_inc(onehots_made, 1)
                dve.wait_ge(perm_made, B)
                nc.vector.tensor_tensor(t["idx"][:R], ST[1][:R, 0, 0:B * NTALL].rearrange("p (b i) -> p b i", b=B),
                                        t["boff"][:R], ALU.add).then_inc(idx_made, 1)
                nc.vector.memset(t["ops"][DK:P, :, OPX, :].bitcast(F32), 0.0)
                nc.vector.memset(t["ops"][DK:P, :, OPY, :].bitcast(F32), 0.0).then_inc(place_step, 1)
                chain += 1
                dve.wait_ge(place_step, chain)
                nc.vector.memset(t["ops"][DK:DK + 1, :, OPY, :].bitcast(F32), 1.0).then_inc(ops_cleared, 1)

                def masks(b, par):
                    n = n_all[:, bass.ds(b, 1)]
                    j = t["jidx"][:, 0:NT]
                    at_least(dve, exp_done, NT * HEADS * (b - 1))
                    nc.vector.tensor_scalar(t["valid"][:, par, :], j, n, None, ALU.is_lt).then_inc(mask_step, 1)
                    nc.vector.tensor_scalar(t["inv"][:, par, :], j, n, None, ALU.is_ge).then_inc(mask_step, 1)
                    nc.vector.tensor_scalar(t["kbias"][:, par, :], j, n, NEG, ALU.is_ge, ALU.mult).then_inc(mask_step, 1)
                    dve.wait_ge(mask_step, 3 * (b + 1))

                def zero_masked(b, par, k):
                    at_least(dve, gathered, 16 * NT * (b + 1))
                    at_least(dve, xT_ready, NT * b + k + 1 - f.NA)
                    nc.vector.tensor_scalar(t["xv"][:R, k % f.NA, :], t["xg"][:R, par, k, :], t["valid"][:R, par, k:k + 1],
                                            None, ALU.mult).then_inc(xv_done, 1)

                def sum_tokens(b, par, k):
                    acc, r = t["xsum"], f.rows(k)
                    if k == 1:
                        at_least(dve, gathered, 16 * NT * (b + 1))
                        at_least(dve, gathered_tail, 16 * f.NTAIL * (b + 1))
                        at_least(dve, xbar_ready, b)
                        other = t["xg"][:R, par, 0, :]
                    else:
                        dve.wait_ge(xsum_step, (NTALL - 1) * b + k - 1)
                        other = acc[:r]
                    nc.vector.tensor_tensor(acc[:r], other, t["xg"][:r, par, k, :], ALU.add).then_inc(xsum_step, 1)

                def reduce_max(s, h, m):
                    dve.wait_ge(mx_ready, 2 * NT * s + m + 1)
                    nc.vector.tensor_reduce(t["mxp"][:R, h % 2, m // 2, m % 2:m % 2 + 1], MX[:R, 0:H], AX.X,
                                            ALU.max).then_inc(mx_red, 1)
                    if m == 2 * NT - 1:
                        dve.wait_ge(mx_red, 2 * NT * (s + 1))
                        at_least(dve, mT_ready, s - 1)
                        nc.vector.tensor_reduce(t["mcol"][:R, h % 2, :], t["mxp"][:R, h % 2], AX.X, ALU.max,
                                                negate=True).then_inc(mcol_done, 1)

                def job(name, arg, bank, b, par, s):
                    if name == "mT":
                        h = arg
                        dve.wait_ge(mT_ready, s + 1)
                        at_least(dve, mrow_put[h % 2], 16 * ((HEADS // 2) * b + h // 2))
                        nc.vector.tensor_copy(t["mrow"][:, h % 2, :], MB[bank][:NT, 0:R]).then_inc(mrow_done, 1)
                    elif name == "proj":
                        g, half = arg
                        p = PAIRS * b + g
                        dve.wait_ge(hi_done, 2 * p + half + 1)
                        cols = slice(half * H, half * H + H)
                        nc.vector.tensor_tensor(t["L"][:, g % 2, cols], MB[bank][:, 0:H],
                                                t["H"][:, g % 2, cols].bitcast(F32), ALU.subtract).then_inc(lo_done, 1)
                    elif name == "L":
                        normalise(s, arg % HEADS, b if arg >= 0 else b - 1, bank)
                    elif name == "out":
                        finish_tile(b - 1, 1 - par, arg, bank)
                    elif name == "xT":
                        if arg + 1 < NT:
                            zero_masked(b + 1, 1 - par, arg + 1)

                def normalise(s, h, b, bank):
                    dve.wait_ge(l_ready, s + 1)
                    at_least(dve, ctx_done, s)
                    nc.vector.reciprocal(t["rsum"][:], MB[bank][:, 0:H]).then_inc(rsum_done, 1)
                    dve.wait_ge(rsum_done, s + 1)
                    dve.wait_ge(ct_kept, s + 1)
                    if h == 0:
                        at_least(dve, out_ready, NT * b)
                    for half in range(2):
                        r0 = DK * half
                        last = nc.vector.scalar_tensor_tensor(
                            out=t["ctxT"][DK * (h % 2):DK * (h % 2) + DK, h // 2, half * H:half * H + H],
                            in0=t["rsum"][r0:r0 + DK, :], scalar=1e30, in1=t["ctxraw"][r0:r0 + DK, :],
                            op0=ALU.min, op1=ALU.mult)
                    last.then_inc(ctx_done, 1)

                def finish_tile(b, par, k, bank):
                    xk = t["xg"][:R, par, k, :]
                    dve.wait_ge(out_ready, NT * b + k + 1)
                    dve.wait_ge(w_kept, b + 1)
                    at_least(dve, out_done, NT * b + k)
                    nc.vector.scalar_tensor_tensor(out=t["xsum"][:R], in0=MB[bank][:R, 0:D],
                                                   scalar=t["valid"][:R, par, k:k + 1], in1=xk, op0=ALU.mult,
                                                   op1=ALU.add).then_inc(out_step, 1)
                    dve.wait_ge(out_step, NT * b + k + 1)
                    nc.vector.scalar_tensor_tensor(out=xk, in0=t["w"][:R, par, :], scalar=t["inv"][:R, par, k:k + 1],
                                                   in1=t["xsum"][:R], op0=ALU.mult, op1=ALU.add).then_inc(out_done, 1)

                masks(0, 0)
                zero_masked(0, 0, 0)
                for name, arg, bank, before in plan[0]:
                    if name == "xT":
                        job(name, arg, bank, -1, 1, 0)
                        if arg == NT - 1:
                            for k in range(1, NTALL):
                                sum_tokens(0, 0, k)
                    elif name == "mT":
                        for s in range(2):
                            for m in range(2 * NT):
                                reduce_max(s, s, m)
                            if s == 0:
                                job(name, arg, bank, 0, 0, 0)
                    else:
                        job(name, arg, bank, 0, 0, 0)

                def batch(b, par, table, has_prev, has_next):
                    sums = [list(range(1 + k * 2, min(3 + k * 2, NTALL))) for k in range(NT)]
                    sums[-1] = list(range(1 + (NT - 1) * 2, NTALL))
                    for h in range(HEADS):
                        s = HEADS * b + h
                        for k in range(NT):
                            ahead = h < HEADS - 2 or has_next
                            if ahead:
                                reduce_max(s + 2, h + 2, 2 * k)
                            for name, arg, bank, before in table[h, k]:
                                job(name, arg, bank, b, par, s + 1 if name == "mT" else s - 1)
                            if ahead:
                                reduce_max(s + 2, h + 2, 2 * k + 1)
                            if has_next and h == 2 and k == 2:
                                masks(b + 1, 1 - par)
                            if has_next and h == 3 and k == 2:
                                zero_masked(b + 1, 1 - par, 0)
                            if has_next and h == 4:
                                for i in sums[k]:
                                    sum_tokens(b + 1, 1 - par, i)

                def tail(jobs):
                    for name, arg, bank, before in jobs:
                        job(name, arg, bank, B, B % 2, HEADS * B - 1)

                run_batches(dve, f, plan, batch, tail)

            either_form(dve, body)

        @block.tensor
        def _(pe):
            pe.wait_ge(consts_made, 7)
            pe.wait_ge(mask_cast, 1)
            for tt in range(TT):
                for u in range(tt + 1):
                    nc.tensor.matmul(ST[0][:, 0, B * tt:B * tt + B], tri[:] if u == tt else ones_b[:], mask_b[:, u, :],
                                     start=(u == 0), stop=(u == tt))
            for u in range(TT):
                last = nc.tensor.matmul(ST[0][:, 1, 0:B], ones_b[:], mask_b[:, u, :], start=(u == 0), stop=(u == TT - 1))
            last.then_inc(counted, 1)
            pe.wait_ge(loaded, 48)
            for k in range(KD):
                at_least(pe, g_kept, k - 1)
                for m in range(KD):
                    last = nc.tensor.matmul(MB[k % 2][:, 0:D], wq_sb[:, m, P * k:P * k + P], woT_sb[:, m, :],
                                            start=(m == 0), stop=(m == KD - 1))
                last.then_inc(g_made, 1)

            def body(f, t, plan):
                NT, R, C, H, NTALL = f.NT, f.R, f.C, f.H, f.NTALL

                pe.wait_ge(onehots_made, TT + 1)
                with pe.Fori(0, B) as b:
                    for tt in range(TT):
                        last = nc.tensor.matmul(ST[1][:R, 0, bass.ds(b * NTALL, NTALL)], t["hot_row"][:, tt, b, :],
                                                t["hot_tile"][:, tt, b, :], start=(tt == 0), stop=(tt == TT - 1))
                    last.then_inc(perm_made, 1)
                pe.wait_ge(g_kept, KD)

                def tile_cols(i):
                    return slice(R * i, R * i + R)

                def half_cols(i):
                    return slice(H * i, H * i + H)

                def max_scores(s, s4, h, m):
                    ops = t["ops"][:, h % SLOTS]
                    if m == 0:
                        pe.wait_ge(dup[h % SLOTS], 96 * (s4 + 1))
                    at_least(pe, mx_red, 2 * NT * s + m)
                    nc.tensor.matmul(MX[:R, 0:H], ops[:, OPA, tile_cols(m // 2)], ops[:, OPB, half_cols(m % 2)],
                                     start=True, stop=True).then_inc(mx_ready, 1)

                def scores(s, s2, h, k):
                    ops, n = t["ops"][:, h % SLOTS], NT * s + k
                    st = ST[(NT * h + k) % 2]
                    if k == 0:
                        pe.wait_ge(mrow_put[h % 2], 16 * (s2 + 1))
                    at_least(pe, exp_done, n - 1)
                    for half in range(2):
                        nc.tensor.matmul(st[:R, half, 0:H], ops[:, OPA, tile_cols(k)], ops[:, OPB, half_cols(half)],
                                         start=True, stop=False)
                    for half in range(2):
                        last = nc.tensor.matmul(st[:R, half, 0:H], ops[:, OPY, tile_cols(k)],
                                                ops[:, OPX, half_cols(half)], start=False, stop=True)
                    last.then_inc(s_ready, 1)

                def times_values(s, p, h, k):
                    if k == 0:
                        at_least(pe, ct_kept, s)
                        at_least(pe, v_kept, 2 * p + 2)
                    pe.wait_ge(exp_done, NT * s + k + 1)
                    for half in range(2):
                        last = nc.tensor.matmul(CT[DK * half:DK * half + DK, 0:H],
                                                t["V"][:R, (h // 2) % 2, k, DK * (h % 2):DK * (h % 2) + DK],
                                                t["Pt"][:R, (NT * h + k) % f.NP, half, :],
                                                start=(k == 0), stop=(k == NT - 1))
                    last.then_inc(pv_done, 1)

                def bank_left(name, arg, b):
                    if name == "xT":
                        at_least(pe, xT_kept, NT * (b + 1) + arg + 1)
                    elif name == "xbar":
                        at_least(pe, xbar_kept, b + 2)
                    elif name == "w":
                        at_least(pe, w_kept, b + 2)
                    elif name == "proj":
                        at_least(pe, lo_done, 2 * (PAIRS * b + arg[0]) + arg[1] + 1)
                    elif name == "V":
                        at_least(pe, v_kept, 2 * (PAIRS * b + arg[0]) + arg[1] + 1)
                    elif name == "mT":
                        at_least(pe, mrow_done, HEADS * b + arg + 1)
                    elif name == "L":
                        at_least(pe, rsum_done, HEADS * b + arg + 1)
                    elif name == "out":
                        at_least(pe, out_step, NT * (b - 1) + arg + 1)

                def job(name, arg, bank, before, b, s):
                    mb = MB[bank]
                    if before:
                        bank_left(before[0], before[1], b + before[2])
                    if name == "xT":
                        pe.wait_ge(xv_done, NT * (b + 1) + arg + 1)
                        for c in range(KD):
                            last = nc.tensor.transpose(mb[:, R * c:R * c + R], t["xv"][:R, arg % f.NA, P * c:P * c + P],
                                                       ident[:R, :R])
                        last.then_inc(xT_ready, 1)
                    elif name == "xbar":
                        pe.wait_ge(xsum_step, (NTALL - 1) * (b + 2))
                        for c in range(KD):
                            last = nc.tensor.matmul(mb[:, P * c:P * c + P], t["xsum"][:R, P * c:P * c + P], meanT[:R, :],
                                                    start=True, stop=True)
                        last.then_inc(xbar_ready, 1)
                    elif name == "w":
                        pe.wait_ge(xbar_kept, b + 2)
                        for c in range(KD):
                            last = nc.tensor.matmul(mb[:, 0:D], t["xbarT"][:, c, :], G[:, c, :],
                                                    start=(c == 0), stop=(c == KD - 1))
                        last.then_inc(w_ready, 1)
                    elif name == "proj":
                        g, half = arg
                        pe.wait_ge(xT_kept, NT * (b + g // PAIRS + 1))
                        for c in range(KD):
                            last = nc.tensor.matmul(mb[:, 0:H], wqT_sb[:, c, P * (g % PAIRS):P * (g % PAIRS) + P],
                                                    t["xcT"][:, c, half_cols(half)], start=(c == 0), stop=(c == KD - 1))
                        last.then_inc(proj_ready, 1)
                    elif name == "V":
                        g, part = arg
                        pe.wait_ge(lo_done, 2 * (PAIRS * b + g) + 2)
                        for i in range(min(4, NT - 4 * part)):
                            cols = tile_cols(4 * part + i)
                            nc.tensor.matmul(mb[:R, P * i:P * i + P], t["H"][:, g % 2, cols], identR[:],
                                             start=True, stop=False)
                            last = nc.tensor.matmul(mb[:R, P * i:P * i + P], t["L"][:, g % 2, cols], identR[:],
                                                    start=False, stop=True)
                        last.then_inc(v_ready, 1)
                    elif name == "mT":
                        pe.wait_ge(mcol_done, s + 1)
                        nc.tensor.transpose(mb[:NT, 0:R], t["mcol"][:R, arg % 2, :], ident[:R, :R]).then_inc(mT_ready, 1)
                    elif name == "L":
                        pe.wait_ge(pacc_step, (NT - 1) * (s + 1))
                        for half in range(2):
                            last = nc.tensor.matmul(mb[DK * half:DK * half + DK, 0:H], ones64[:R, :],
                                                    t["Pacc"][:R, arg % HEADS % f.NA, half, :], start=True, stop=True)
                        last.then_inc(l_ready, 1)
                    elif name == "out":
                        pe.wait_ge(ctx_done, HEADS * b)
                        for c in range(KD):
                            last = nc.tensor.matmul(mb[:R, 0:D], t["ctxT"][:, c, tile_cols(arg)], woT_sb[:, c, :],
                                                    start=(c == 0), stop=(c == KD - 1))
                        last.then_inc(out_ready, 1)

                for (name, arg, bank, before), (_, _, b) in zip(plan[0], front_jobs(f)):
                    if before:
                        bank_left(*before)
                    if name == "mT":
                        for m in range(2 * NT):
                            max_scores(0, 0, 0, m)
                    job(name, arg, bank, None, b, 0)
                for m in range(2 * NT):
                    max_scores(1, 0, 1, m)

                def batch(b, par, table, has_prev, has_next):
                    for h in range(HEADS):
                        s = HEADS * b + h
                        for k in range(NT):
                            ahead = h < HEADS - 2 or has_next
                            if ahead:
                                max_scores(s + 2, 2 * b + (h + 2) // SLOTS, h + 2, 2 * k)
                            scores(s, (HEADS // 2) * b + h // 2, h, k)
                            for name, arg, bank, before in table[h, k]:
                                job(name, arg, bank, before, b, s + 1 if name == "mT" else s - 1)
                            if ahead:
                                max_scores(s + 2, 2 * b + (h + 2) // SLOTS, h + 2, 2 * k + 1)
                            if k > 0:
                                times_values(s, PAIRS * b + h // 2, h, k - 1)
                            elif h > 0:
                                times_values(s - 1, PAIRS * b + (h - 1) // 2, h - 1, NT - 1)
                            elif has_prev:
                                times_values(s - 1, PAIRS * b - 1, HEADS - 1, NT - 1)

                def tail(jobs):
                    times_values(HEADS * B - 1, PAIRS * B - 1, HEADS - 1, NT - 1)
                    for name, arg, bank, before in jobs:
                        job(name, arg, bank, before, B, HEADS * B - 1)

                run_batches(pe, f, plan, batch, tail)

            either_form(pe, body)


def kernel(x, cond_2048, L0_cond_Wq, L0_cond_Wo):
    import numpy as np
    import concourse.bacc as bacc
    from concourse.bass_utils import run_bass_kernel_spmd

    x = np.asarray(x)
    B, D, T = x.shape
    mask = np.asarray(cond_2048)
    wq, wo = np.asarray(L0_cond_Wq), np.asarray(L0_cond_Wo)
    arrays = {
        "x_rows": np.ascontiguousarray(x.transpose(0, 2, 1)).reshape(B * T, D),
        "mask_t": np.ascontiguousarray(mask.reshape(B, T // P, P).transpose(2, 1, 0)).reshape(P, -1),
        "wq": np.ascontiguousarray(wq),
        "wqT": np.ascontiguousarray(wq.T),
        "woT": np.ascontiguousarray(wo.T),
    }
    nc = bacc.Bacc("TRN2", target_bir_lowering=False, num_devices=1)
    ins = [nc.dram_tensor(n, a.shape, F32, kind="ExternalInput").ap() for n, a in arrays.items()]
    out = nc.dram_tensor("out_rows", (B * T, D), F32, kind="ExternalOutput").ap()
    attention_kernel(nc, *ins, out, B, T, D)
    got = run_bass_kernel_spmd(nc, [arrays], core_ids=[0]).results[0]["out_rows"]
    return np.ascontiguousarray(got.reshape(B, T, D).transpose(0, 2, 1))
```

```python
from contextlib import ExitStack

import concourse.bass as bass
from concourse import mybir

P = 128
F32 = mybir.dt.float32
F32R = mybir.dt.float32r
BF16 = mybir.dt.bfloat16
F16 = mybir.dt.float16
I32 = mybir.dt.int32
ALU = mybir.AluOpType
ACT = mybir.ActivationFunctionType
AX = mybir.AxisListType

HEADS = 8
DK = 64
PAIRS = HEADS // 2
NEG = -1e30
SLOTS = 4
OPA, OPB, OPY, OPX = range(4)


class Form:

    def __init__(self, name, NT, R, T, NP, NA, NC, keeps_q):
        self.name, self.NT, self.R, self.T = name, NT, R, T
        self.C = NT * R
        self.H = self.C // 2
        self.NTALL = -(-T // R)
        self.RL = T - R * (self.NTALL - 1)
        self.NTAIL = self.NTALL - NT
        self.NP, self.NA, self.NC = NP, NA, NC
        self.late_scale = NT < 6
        self.keeps_q = keeps_q

    def rows(self, k):
        return self.RL if k == self.NTALL - 1 else self.R


def misc_jobs(form, has_prev, has_next):
    NT = form.NT
    table = {(h, k): [] for h in range(HEADS) for k in range(NT)}
    for h in range(HEADS):
        if h % 2 == 1 and (h < 7 or has_next):
            table[h, 0].append(("V", ((h + 1) // 2, 0)))
            table[h, 1].append(("V", ((h + 1) // 2, 1)))
        if h > 0 or has_prev:
            table[h, 2].append(("L", h - 1))
    for at, pair in (((0, 3), (2, 1)), ((1, 3), (3, 0)), ((2, 3), (3, 1)), ((4, 1), (4, 0)), ((4, 3), (4, 1)),
                     ((5, 3), (5, 0)), ((6, 3), (5, 1)), ((7, 3), (6, 0))):
        if at < (4, 0) or has_next:
            table[at].append(("proj", pair))
    if has_prev:
        for k, at in enumerate(out_steps(form)):
            table[at].append(("out", k))
    if has_next:
        for k in range(NT):
            table[3, k].append(("xT", k))
        table[6, 0].append(("xbar", 0))
        table[6, 1].append(("w", 0))
    for h in range(HEADS - 1 + has_next):
        table[h, 0].append(("mT", h + 1))
    for jobs in table.values():
        assert all(name not in TWO_PARTS for name, _ in jobs[:-2])
    return table


TWO_PARTS = ("proj", "out", "w")
LATE = ("proj", "out", "w", "mT")


def out_steps(form):
    return [(1, 1), (1, 3), (1, 4), (2, 0), (2, 2)] if form.NT == 5 else \
        [(0, 5), (0, 5), (0, 6), (0, 6), (0, 7), (0, 7), (1, 1), (1, 3)]


def pool_jobs(form, has_prev, has_next):
    NT, NTAIL = form.NT, form.NTAIL
    table = {(h, k): [] for h in range(HEADS) for k in range(NT)}
    steps = list(table)
    scatters = [steps[steps.index(at) + 2] for at in out_steps(form)]
    gathers = [max(steps[steps.index(at) + 2], (1, 4)) for at in scatters]
    if has_prev:
        for i, at in enumerate(scatters):
            table[at].append(("scatter", i))
    else:
        for i in range(NTAIL):
            table[steps[2 * NT + i]].append(("add_w_first", i))
            table[steps[3 * NT + i]].append(("scatter_tail_first", i))
    if has_next:
        for i in range(NTAIL):
            table[steps[1 + i]].append(("gather", NT + i))
            table[[(6, 3), (6, 4), (7, 0), (7, 1), (7, 2)][i]].append(("add_w", i))
            table[7, min(3 + i // 2, 4)].append(("scatter_tail", i))
        for i in range(NT):
            table[gathers[i]].append(("gather", i))
    return table


def vector_jobs(form, has_prev, has_next):
    table = {(h, k, a): [] for h in range(HEADS) for k in range(form.NT) for a in range(2)}
    for h in range(HEADS):
        if h > 0 or has_prev:
            for quarter, at in enumerate([(2, 1), (3, 0), (3, 1), (4, 0)]):
                table[(h, *at)].append(("reciprocal", quarter))
            table[h, 4, 1].append(("scale", 0))
            if not form.late_scale:
                table[h, 4, 1].append(("scale", 1))
        if form.late_scale and (h > 1 or has_prev):
            table[h, 0, 0].append(("scale", 1))
    if has_next:
        table[2, 3, 1].append(("masks", 0))
        table[2, 4, 1].append(("zero_masked", 0))
        steps = [(h, *at) for h in (4, 5) for at in ((0, 1), (1, 0), (1, 1), (2, 0), (3, 0))]
        for i in range(1, form.NTALL):
            table[steps[i - 1]].append(("sum_tokens", i))
    return table


def front_jobs(form):
    return ([("xT", k, -1) for k in range(form.NT)] + [("proj", (0, 0), 0), ("proj", (0, 1), 0)]
            + [("V", (0, 0), 0), ("V", (0, 1), 0), ("proj", (1, 0), 0), ("proj", (1, 1), 0)]
            + [("proj", (2, 0), 0), ("mT", 0, 0), ("xbar", 0, -1), ("w", 0, -1)])


def tail_jobs(form):
    return [("L", -1, 0)] + [("out", k, 0) for k in range(form.NT)]


def with_banks(form):
    def give(jobs, start, two_back):
        out = []
        for i, (name, arg, back) in enumerate(jobs):
            out.append((name, arg, (start + i) % 2, two_back[-2]))
            two_back = [two_back[-1], (name, arg, back)]
        return out, two_back

    def give_table(table, start, two_back):
        steps = list(table)
        flat, two_back = give([(*job, 0) for at in steps for job in table[at]], start, two_back)
        flat = iter(flat)
        return {at: [next(flat) for _ in table[at]] for at in steps}, two_back

    def one_later(two_back):
        return [(name, arg, back - 1) for name, arg, back in two_back]

    def count(table):
        return sum(map(len, table.values()))

    tables = [misc_jobs(form, False, True), misc_jobs(form, True, True), misc_jobs(form, True, False)]
    assert count(tables[1]) % 2 == 0
    front, end = give(front_jobs(form), 0, [None, None])
    at = len(front)
    first, end = give_table(tables[0], at, end)
    at += count(tables[0])
    mid, same_end = give_table(tables[1], at, one_later(end))
    assert same_end == end
    last, end = give_table(tables[2], at, one_later(end))
    tail, _ = give(tail_jobs(form), at + count(tables[2]), one_later(end))
    return front, first, mid, last, tail


def at_least(eng, sem, value):
    if not isinstance(value, int) or value > 0:
        eng.wait_ge(sem, value)


def wait_alone(eng, sem, value, passed):
    if not isinstance(value, int) or value > 0:
        eng.wait_ge(sem, value)
        eng.sem_inc(passed, 1)


def attention_kernel(nc, x_rows, mask_t, wq, wqT, woT, out_rows, B, T, D):
    KD = D // P
    TT = T // P
    forms = [Form("small", 5, 108, T, 4, 2, 2, True), Form("middle", 5, 116, T, 4, 2, 2, True), Form("full", 8, 128, T, 2, 1, 1, False)]
    SCALE = float(DK) ** -0.5

    with ExitStack() as ctx:
        def sb(name, shape, dt, stack=ctx):
            return stack.enter_context(nc.sbuf_tensor(name, shape, dt))

        def psum(name, shape, dt):
            return ctx.enter_context(nc.psum_tensor(name, shape, dt))

        def sem(name):
            return ctx.enter_context(nc.semaphore(name))

        ST = [psum(f"scores{i}", [P, 512], F32) for i in range(3)]
        MX = [psum(f"max_scores{i}", [P, 512], F32) for i in range(2)]
        CT = psum("ctx_psum", [P, 512], F32)
        MB = [psum(f"misc{i}", [P, 512], F32) for i in range(2)]

        wqT_sb = sb("wqT_sb", [P, KD, D], F32)
        woT_sb = sb("woT_sb", [P, KD, D], F32)
        G = sb("G", [P, KD, D], F32)
        ident = sb("ident", [P, P], F32)
        identR = sb("identR", [P, P], F32R)
        ones64 = sb("ones64", [P, DK], F32)
        tiny = sb("tiny", [P, 1], F32)
        meanT = sb("meanT", [P, P], F32)
        n_all = sb("n_all", [P, B], F32)
        n_max = sb("n_max", [P, 1], F32)
        n_max_i = sb("n_max_i", [P, 1], I32)
        pos = sb("pos", [P, TT, B], F32)
        tokid = sb("tokid", [P, TT, B], F32)

        sems = {n: sem(n) for n in (
            "loaded mask_loaded consts_made iotas_made consts_cast mask_cast counted pos_step pos_done g_made g_kept "
            "place_step onehots_made perm_made idx_made jidx_made ops_cleared").split()}
        loaded, mask_loaded, consts_made, iotas_made, consts_cast, mask_cast, counted, pos_step, pos_done, g_made, \
            g_kept, place_step, onehots_made, perm_made, idx_made, jidx_made, ops_cleared = sems.values()
        s_ready, mx_ready, pv_done = sem("s_ready"), sem("mx_ready"), sem("pv_done")
        xT_ready, xbar_ready, w_ready = sem("xT_ready"), sem("xbar_ready"), sem("w_ready")
        proj_ready, v_ready, mT_ready = sem("proj_ready"), sem("v_ready"), sem("mT_ready")
        l_ready, out_ready = sem("l_ready"), sem("out_ready")
        exp_done, xT_kept, hi_done, v_kept = sem("exp_done"), sem("xT_kept"), sem("hi_done"), sem("v_kept")
        xbar_kept, w_kept, ct_kept, q_kept = sem("xbar_kept"), sem("w_kept"), sem("ct_kept"), sem("q_kept")
        mx_red, mcol_done, mrow_done, lo_done = sem("mx_red"), sem("mcol_done"), sem("mrow_done"), sem("lo_done")
        ctx_done, xv_done, xsum_step, mask_step = sem("ctx_done"), sem("xv_done"), sem("xsum_step"), sem("mask_step")
        out_step, out_done, rsum_done = sem("out_step"), sem("out_done"), sem("rsum_done")
        recip_step = sem("recip_step")
        pacc_step, idx_copied, tail_added = sem("pacc_step"), sem("idx_copied"), sem("tail_added")
        sp_passed, pool_passed = sem("sp_passed"), sem("pool_passed")
        dup = [sem(f"dup{i}") for i in range(SLOTS)]
        mrow_put = [sem(f"mrow_put{i}") for i in range(2)]
        gathered = [sem(f"gathered{i}") for i in range(TT)]
        scattered = [sem(f"scattered{i}") for i in range(TT)]
        gathered_tail = sem("gathered_tail")
        scattered_tail = [sem(f"scattered_tail{i}") for i in range(2)]

        start = ExitStack()
        mask_f = sb("mask_f", [P, TT, B], F32, start)
        mask_b = sb("mask_b", [P, TT, B], BF16, start)
        tri = sb("tri", [P, P], BF16, start)
        ones_b = sb("ones_b", [P, P], BF16, start)
        cnt = sb("cnt", [P, TT, B], F32, start)
        behind = sb("behind", [P, TT, B], F32, start)
        tokid_i = sb("tokid_i", [P, TT, B], I32, start)
        start.close()

        tensors = [{} for _ in forms]
        for f, t in zip(forms, tensors):
            own = ExitStack()

            def keep(name, shape, dt, stack=own, t=t, f=f):
                t[name] = sb(f"{f.name}_{name}", shape, dt, stack)

            keep("xg", [P, 2, f.NTALL, D], F32)
            keep("xcT", [P, KD, f.C], F32)
            keep("idx", [P, B, f.NTALL], I32)
            keep("jidx", [P, f.NTALL], F32)
            keep("idx_cur", [P, 2, f.NTALL], I32)
            keep("valid", [P, 2, f.NT], F32)
            keep("inv", [P, 2, f.NT], F32)
            keep("kbias", [P, 2, f.NT], F32)
            tables = ExitStack()
            t["jh"] = sb(f"{f.name}_jh", [P, TT, B], F32, tables)
            t["jl"] = sb(f"{f.name}_jl", [P, TT, B], F32, tables)
            t["tileno"] = sb(f"{f.name}_tileno", [P, f.NTALL], F32, tables)
            t["tileno_i"] = sb(f"{f.name}_tileno_i", [P, f.NTALL], I32, tables)
            t["rowno"] = sb(f"{f.name}_rowno", [P, f.R], F32, tables)
            t["rowno_i"] = sb(f"{f.name}_rowno_i", [P, f.R], I32, tables)
            t["jidx_i"] = sb(f"{f.name}_jidx_i", [P, f.NTALL], I32, tables)
            t["boff_i"] = sb(f"{f.name}_boff_i", [P, B, f.NTALL], I32, tables)
            t["boff"] = sb(f"{f.name}_boff", [P, B, f.NTALL], F32, tables)
            t["hot_tile_f"] = sb(f"{f.name}_hot_tile_f", [P, TT, B, f.NTALL], F32, tables)
            t["hot_tile"] = sb(f"{f.name}_hot_tile", [P, TT, B, f.NTALL], F16, tables)
            t["hot_row"] = sb(f"{f.name}_hot_row", [P, TT, B, f.R], F16, tables)
            tables.close()
            keep("ops", [P, SLOTS, 4, f.C], F32R)
            keep("H", [P, 2, f.C], F32R)
            keep("L", [P, 2, f.C], F32R)
            if f.keeps_q:
                keep("Q", [P, 2, f.C], F32)
            keep("V", [P, 2, f.NT, P], F32)
            keep("Pt", [P, f.NP, 2, f.H], F32)
            keep("Pacc", [P, f.NA, 2, f.H], F32)
            keep("ctxraw", [P, f.H], F32)
            keep("rsum", [P, f.H], F32)
            keep("w", [P, 2, D], F32)
            keep("xbarT", [P, KD, P], F32)
            keep("xsum", [P, D], F32)
            keep("xv", [P, f.NA, D], F32)
            keep("mxp", [P, 2, f.NT, 2], F32)
            keep("mcol", [P, 2, f.NT], F32)
            keep("mrow", [f.NT, 2, f.R], F32R)
            if f is forms[-1]:
                over = ExitStack()
                wq_sb = sb("wq_sb", [P, KD, D], F32, over)
                over.close()
            keep("ctxT", [P, f.NC, KD, f.C], F32)
            own.close()

        block = ctx.enter_context(nc.Block())
        plans = [with_banks(f) for f in forms]

        def run_batches(eng, form, plan, batch, tail):
            front, first, mid, last, tail_plan = plan
            batch(0, 0, first, False, True)
            batch(1, 1, mid, True, True)
            with eng.Fori(2, B - 2, 2) as b:
                batch(b, 0, mid, True, True)
                batch(b + 1, 1, mid, True, True)
            batch(B - 2, 0, mid, True, True)
            batch(B - 1, 1, last, True, False)
            tail(tail_plan)

        def fitting_form(eng, body):
            eng.wait_ge(pos_done, 2)
            n = eng.value_load(n_max_i[0:1, 0:1], min_val=0, max_val=T)
            with eng.If(n <= forms[0].C):
                body(forms[0], tensors[0], plans[0])
            with eng.Else():
                with eng.If(n <= forms[1].C):
                    body(forms[1], tensors[1], plans[1])
                with eng.Else():
                    body(forms[2], tensors[2], plans[2])

        @block.sync
        def _(sp):
            sp.dma_start(mask_f[:].rearrange("p t b -> p (t b)"), mask_t).then_inc(mask_loaded, 16)
            for dst, src in ((wq_sb, wq), (woT_sb, woT), (wqT_sb, wqT)):
                sp.dma_start(dst[:], src.rearrange("(k p) n -> p k n", p=P)).then_inc(loaded, 16)

            def body(f, t, plan):
                NT, R = f.NT, f.R

                def copy_operands(s, h):
                    slot, r0, stage = h % SLOTS, DK * (h % 2), (h // 2) % 2
                    hi = t["H"][r0:r0 + DK, stage, :]
                    lo = t["L"][r0:r0 + DK, stage, :]
                    wait_alone(sp, lo_done, s - h % 2 + 2, sp_passed)
                    wait_alone(sp, s_ready, 2 * NT * (s - SLOTS + 1), sp_passed)
                    for op, half, src in ((OPA, 0, hi), (OPA, 1, lo), (OPB, 0, hi), (OPB, 1, hi), (OPY, 0, hi),
                                          (OPX, 0, lo)):
                        sp.dma_start(t["ops"][DK * half:DK * half + DK, slot, op, :].bitcast(F32),
                                     src.bitcast(F32)).then_inc(dup[slot], 16)

                def put_max_row(s, h):
                    wait_alone(sp, mrow_done, s + 1, sp_passed)
                    sp.dma_start(t["ops"][DK:DK + 1, h % SLOTS, OPX, :].bitcast(F32).rearrange("o (k r) -> o k r", r=R),
                                 t["mrow"][:, h % 2, :].bitcast(F32)).then_inc(mrow_put[h % 2], 16)

                sp.wait_ge(ops_cleared, 3)
                copy_operands(0, 0)
                copy_operands(1, 1)
                copy_operands(2, 2)
                put_max_row(0, 0)

                def batch(b, par, table, has_prev, has_next):
                    for h in range(HEADS):
                        s = HEADS * b + h
                        if h < HEADS - 1 or has_next:
                            put_max_row(s + 1, h + 1)
                        if h < HEADS - 3 or has_next:
                            copy_operands(s + 3, h + 3)

                run_batches(sp, f, plan, batch, lambda tail: None)

            fitting_form(sp, body)

        @block.gpsimd
        def _(pool):
            nc.gpsimd.memset(ident[:], 0.0).then_inc(consts_made, 1)
            nc.gpsimd.memset(tri[:], 1.0).then_inc(consts_made, 1)
            nc.gpsimd.memset(ones_b[:], 1.0).then_inc(consts_made, 1)
            nc.gpsimd.memset(ones64[:], 1.0).then_inc(consts_made, 1)
            nc.gpsimd.memset(meanT[:], 1.0 / T).then_inc(consts_made, 1)
            nc.gpsimd.memset(tiny[:], 1e-30).then_inc(consts_made, 1)
            pool.wait_ge(consts_made, 6)
            nc.gpsimd.affine_select(out=ident[:], in_=ident[:], compare_op=ALU.not_equal, fill=1.0, base=0,
                                    pattern=[[-1, P]], channel_multiplier=1).then_inc(consts_made, 1)
            nc.gpsimd.affine_select(out=tri[:], in_=tri[:], compare_op=ALU.is_ge, fill=0.0, base=0,
                                    pattern=[[1, P]], channel_multiplier=-1).then_inc(consts_made, 1)
            nc.gpsimd.iota(tokid_i[:], pattern=[[P, TT], [0, B]], base=0, channel_multiplier=1).then_inc(iotas_made, 1)

            def body(f, t, plan):
                NT, R, NTALL, NTAIL = f.NT, f.R, f.NTALL, f.NTAIL
                nc.gpsimd.iota(t["tileno_i"][:], pattern=[[1, NTALL]], base=0, channel_multiplier=0).then_inc(iotas_made, 1)
                nc.gpsimd.iota(t["rowno_i"][:], pattern=[[1, R]], base=0, channel_multiplier=0).then_inc(iotas_made, 1)
                nc.gpsimd.iota(t["jidx_i"][:], pattern=[[R, NTALL]], base=0, channel_multiplier=1).then_inc(iotas_made, 1)
                nc.gpsimd.iota(t["boff_i"][:], pattern=[[T, B], [0, NTALL]], base=0, channel_multiplier=0).then_inc(iotas_made, 1)
                def copy_order(b, par, k):
                    copies = NT + (1 if NTAIL else 0)
                    if k == NT:
                        at_least(pool, scattered_tail[par], 8 * NTAIL * (b - par))
                        nc.gpsimd.tensor_copy(t["idx_cur"][:R, par, NT:], t["idx"][:R, b, NT:]).then_inc(idx_copied, 1)
                        wait_alone(pool, idx_copied, copies * b + 1, pool_passed)
                    if k < NT:
                        at_least(pool, scattered[k], 16 * (b - 1))
                        nc.gpsimd.tensor_copy(t["idx_cur"][:R, par, k:k + 1],
                                              t["idx"][:R, b, k:k + 1]).then_inc(idx_copied, 1)
                        wait_alone(pool, idx_copied, copies * b + copies - NT + k + 1, pool_passed)

                def gather(b, par, k):
                    r = f.rows(k)
                    nc.gpsimd.indirect_dma_start(
                        out=t["xg"][:r, par, k, :], out_offset=None, in_=x_rows,
                        in_offset=bass.IndirectOffsetOnAxis(ap=t["idx_cur"][:r, par, k:k + 1], axis=0),
                    ).then_inc(gathered[k] if k < NT else gathered_tail, 16)

                def scatter(par, k, done):
                    r = f.rows(k)
                    nc.gpsimd.indirect_dma_start(
                        out=out_rows, in_=t["xg"][:r, par, k, :], in_offset=None,
                        out_offset=bass.IndirectOffsetOnAxis(ap=t["idx_cur"][:r, par, k:k + 1], axis=0),
                    ).then_inc(done, 16)

                def add_w(b, par, i):
                    if i == 0:
                        at_least(pool, w_kept, b + 1)
                        at_least(pool, xsum_step, (NTALL - 1) * (b + 1))
                    r, xk = f.rows(NT + i), t["xg"][:, par, NT + i, :]
                    nc.gpsimd.tensor_tensor(xk[:r], xk[:r], t["w"][:r, par, :], ALU.add).then_inc(tail_added, 1)

                def scatter_tail(b, par, i):
                    if i == 0:
                        wait_alone(pool, tail_added, NTAIL * (b + 1), pool_passed)
                    scatter(par, NT + i, scattered_tail[par])

                def job(name, arg, b, par):
                    if name == "scatter":
                        wait_alone(pool, out_done, NT * (b - 1) + arg + 1, pool_passed)
                        scatter(1 - par, arg, scattered[arg])
                    elif name == "gather":
                        if arg <= NT:
                            copy_order(b + 1, 1 - par, arg)
                        gather(b + 1, 1 - par, arg)
                    elif name == "add_w":
                        add_w(b + 1, 1 - par, arg)
                    elif name == "scatter_tail":
                        scatter_tail(b + 1, 1 - par, arg)
                    elif name == "add_w_first":
                        add_w(b, par, arg)
                    elif name == "scatter_tail_first":
                        scatter_tail(b, par, arg)

                def add_tile(s, h, k):
                    acc, p0 = t["Pacc"][:R, h % f.NA], (NT * h + k) % f.NP
                    if k == 1:
                        at_least(pool, l_ready, s - f.NA + 1)
                        other = t["Pt"][:R, (NT * h) % f.NP]
                    else:
                        pool.wait_ge(pacc_step, (NT - 1) * s + k - 1)
                        other = acc
                    pool.wait_ge(exp_done, 2 * (NT * s + k) + 2)
                    nc.gpsimd.tensor_tensor(acc, other, t["Pt"][:R, p0], ALU.add).then_inc(pacc_step, 1)

                pool.wait_ge(idx_made, 1)
                if NTAIL:
                    copy_order(0, 0, NT)
                for k in range(NTALL):
                    if k < NT:
                        copy_order(0, 0, k)
                    gather(0, 0, k)
                pool.wait_ge(idx_made, 2)
                nc.gpsimd.memset(t["ops"][DK:P, :, OPX, :].bitcast(F32), 0.0).then_inc(ops_cleared, 1)
                nc.gpsimd.memset(t["ops"][DK:P, :, OPY, :].bitcast(F32), 0.0).then_inc(ops_cleared, 1)
                pool.wait_ge(ops_cleared, 2)
                nc.gpsimd.memset(t["ops"][DK:DK + 1, :, OPY, :].bitcast(F32), 1.0).then_inc(ops_cleared, 1)

                def batch(b, par, table, has_prev, has_next):
                    jobs = pool_jobs(f, has_prev, has_next)
                    for h in range(HEADS):
                        for k in range(NT):
                            if k > 0:
                                add_tile(HEADS * b + h, h, k)
                            for name, arg in jobs[h, k]:
                                job(name, arg, b, par)

                def tail(jobs):
                    for i in range(NT):
                        pool.wait_ge(out_done, NT * (B - 1) + i + 1)
                        scatter((B - 1) % 2, i, scattered[i])
                    for i in range(NT):
                        pool.wait_ge(scattered[i], 16 * B)
                    for par in range(2):
                        at_least(pool, scattered_tail[par], 8 * NTAIL * B)

                run_batches(pool, f, plan, batch, tail)

            fitting_form(pool, body)

        @block.scalar
        def _(act):
            act.wait_ge(consts_made, 8)
            for k in range(KD):
                act.wait_ge(g_made, k + 1)
                nc.scalar.copy(G[:, k, :], MB[k % 2][:, 0:D]).then_inc(g_kept, 1)

            def body(f, t, plan):
                NT, R, C, H = f.NT, f.R, f.C, f.H

                def job(name, arg, bank, b, par):
                    if name == "xT":
                        act.wait_ge(xT_ready, NT * (b + 1) + arg + 1)
                        at_least(act, proj_ready, 2 * PAIRS * (b + 1))
                        nc.scalar.copy(t["xcT"][:, :, R * arg:R * arg + R],
                                       MB[bank][:, 0:KD * R].rearrange("p (c r) -> p c r", c=KD)).then_inc(xT_kept, 1)
                    elif name == "xbar":
                        act.wait_ge(xbar_ready, b + 2)
                        at_least(act, w_ready, b + 1)
                        nc.scalar.copy(t["xbarT"][:].rearrange("p k n -> p (k n)"), MB[bank][:, 0:KD * P]).then_inc(xbar_kept, 1)
                    elif name == "w":
                        act.wait_ge(w_ready, b + 2)
                        at_least(act, out_done, NT * b)
                        at_least(act, tail_added, f.NTAIL * b)
                        nc.scalar.copy(t["w"][:, 1 - par, :], MB[bank][:, 0:D]).then_inc(w_kept, 1)
                    elif name == "proj":
                        g, half = arg
                        p = PAIRS * b + g
                        act.wait_ge(proj_ready, 2 * p + half + 1)
                        at_least(act, lo_done, 2 * p - 2)
                        at_least(act, dup[(2 * g) % SLOTS], 96 * (2 * b + g // 2))
                        at_least(act, dup[(2 * g + 1) % SLOTS], 96 * (2 * b + g // 2))
                        at_least(act, v_ready, 2 * p - 2)
                        cols = slice(half * H, half * H + H)
                        q = MB[bank][:, 0:H]
                        if f.keeps_q:
                            nc.scalar.copy(t["Q"][:, g % 2, cols], q).then_inc(q_kept, 1)
                            act.wait_ge(q_kept, 2 * p + half + 1)
                            q = t["Q"][:, g % 2, cols]
                        nc.scalar.copy(t["H"][:, g % 2, cols], q).then_inc(hi_done, 1)
                    elif name == "V":
                        g, part = arg
                        p = PAIRS * b + g
                        n = min(4, NT - 4 * part)
                        act.wait_ge(v_ready, 2 * p + part + 1)
                        at_least(act, pv_done, NT * (2 * p - 2))
                        nc.scalar.copy(t["V"][:R, g % 2, 4 * part:4 * part + n, :],
                                       MB[bank][:R, 0:n * P].rearrange("r (k c) -> r k c", k=n)).then_inc(v_kept, 1)

                def keep_sums(s, bank):
                    act.wait_ge(l_ready, s + 1)
                    at_least(act, ctx_done, s)
                    nc.scalar.activation(t["rsum"][:], MB[bank][:, 0:H], ACT.Identity,
                                         bias=tiny[:, 0:1]).then_inc(rsum_done, 1)

                def keep_ctx(s, h):
                    act.wait_ge(pv_done, NT * (s + 1))
                    at_least(act, ctx_done, s)
                    nc.scalar.copy(t["ctxraw"][:], CT[:, 0:H]).then_inc(ct_kept, 1)

                for name, arg, bank, before in plan[0]:
                    job(name, arg, bank, 0 if name in ("proj", "V") else -1, 1)

                def batch(b, par, table, has_prev, has_next):
                    for h in range(HEADS):
                        s = HEADS * b + h
                        for k in range(NT):
                            if k == 1 and (h > 0 or has_prev):
                                keep_ctx(s - 1, h - 1)
                            n = NT * s + k
                            if h == 0 and k == 0:
                                act.wait_ge(mask_step, 3 * (b + 1))
                            at_least(act, pv_done, n - f.NP + 1)
                            ko, so = k - f.NP, s
                            while ko < 0:
                                ko, so = ko + NT, so - 1
                            at_least(act, pacc_step, (NT - 1) * so + max(ko, 1))
                            for half in range(2):
                                act.wait_ge(s_ready, 2 * n + half + 1)
                                nc.scalar.activation(t["Pt"][:R, (NT * h + k) % f.NP, half, :],
                                                     ST[(2 * (NT * h + k) + half) % 3][:R, 0:H], ACT.Exp,
                                                     bias=t["kbias"][:R, par, k:k + 1],
                                                     scale=SCALE).then_inc(exp_done, 1)
                            for name, arg, bank, before in table[h, k]:
                                if name == "L":
                                    keep_sums(s - 1, bank)
                                else:
                                    job(name, arg, bank, b, par)

                def tail(jobs):
                    keep_ctx(HEADS * B - 1, HEADS - 1)
                    keep_sums(HEADS * B - 1, jobs[0][2])

                run_batches(act, f, plan, batch, tail)

            fitting_form(act, body)

        @block.vector
        def _(dve):
            dve.wait_ge(mask_loaded, 16)
            nc.vector.tensor_copy(mask_b[:], mask_f[:]).then_inc(mask_cast, 1)
            dve.wait_ge(iotas_made, 1)
            nc.vector.tensor_copy(tokid[:], tokid_i[:]).then_inc(pos_step, 1)
            dve.wait_ge(consts_made, 8)
            nc.vector.tensor_copy(identR[:], ident[:]).then_inc(consts_cast, 1)
            dve.wait_ge(counted, 1)
            nc.vector.tensor_copy(cnt[:].rearrange("p t b -> p (t b)"), ST[0][:, 0:TT * B]).then_inc(pos_step, 1)
            nc.vector.tensor_copy(n_all[:], ST[1][:, 0:B]).then_inc(pos_step, 1)
            dve.wait_ge(pos_step, 3)
            nc.vector.tensor_tensor(behind[:], tokid[:], cnt[:], ALU.subtract).then_inc(pos_step, 1)
            nc.vector.tensor_reduce(n_max[:], n_all[:], AX.X, ALU.max).then_inc(pos_step, 1)
            dve.wait_ge(pos_step, 5)
            nc.vector.tensor_tensor(behind[:], behind[:], n_all[:].unsqueeze(1).to_broadcast([P, TT, B]),
                                    ALU.add).then_inc(pos_step, 1)
            nc.vector.tensor_copy(n_max_i[:], n_max[:]).then_inc(pos_done, 1)
            dve.wait_ge(pos_step, 6)
            nc.vector.scalar_tensor_tensor(out=cnt[:], in0=cnt[:], scalar=-1.0, in1=behind[:], op0=ALU.add,
                                           op1=ALU.subtract).then_inc(pos_step, 1)
            dve.wait_ge(pos_step, 7)
            nc.vector.tensor_tensor(cnt[:], cnt[:], mask_f[:], ALU.mult).then_inc(pos_step, 1)
            dve.wait_ge(pos_step, 8)
            nc.vector.tensor_tensor(pos[:], cnt[:], behind[:], ALU.add).then_inc(pos_done, 1)

            def body(f, t, plan):
                NT, R, C, H, NTALL = f.NT, f.R, f.C, f.H, f.NTALL
                chain = 0

                dve.wait_ge(iotas_made, 5)
                nc.vector.tensor_copy(t["tileno"][:], t["tileno_i"][:]).then_inc(place_step, 1)
                nc.vector.tensor_copy(t["rowno"][:], t["rowno_i"][:]).then_inc(place_step, 1)
                nc.vector.tensor_copy(t["jidx"][:], t["jidx_i"][:]).then_inc(jidx_made, 1)
                nc.vector.tensor_copy(t["boff"][:], t["boff_i"][:]).then_inc(place_step, 1)
                nc.vector.tensor_scalar(t["jh"][:], pos[:], float(R), None, ALU.is_ge).then_inc(place_step, 1)
                chain = 4
                for i in range(2, NTALL):
                    dve.wait_ge(place_step, chain)
                    nc.vector.scalar_tensor_tensor(out=t["jh"][:], in0=pos[:], scalar=float(R * i), in1=t["jh"][:],
                                                   op0=ALU.is_ge, op1=ALU.add).then_inc(place_step, 1)
                    chain += 1
                dve.wait_ge(place_step, chain)
                nc.vector.scalar_tensor_tensor(out=t["jl"][:], in0=t["jh"][:], scalar=-float(R), in1=pos[:],
                                               op0=ALU.mult, op1=ALU.add).then_inc(place_step, 1)
                hot_shape = [P, TT * B, NTALL]
                flat = lambda a: a[:].rearrange("p t b -> p (t b)").unsqueeze(2).to_broadcast(hot_shape)
                hot_f = t["hot_tile_f"][:].rearrange("p t b i -> p (t b) i")
                nc.vector.tensor_tensor(hot_f, t["tileno"][:].unsqueeze(1).to_broadcast(hot_shape), flat(t["jh"]),
                                        ALU.is_equal).then_inc(place_step, 1)
                chain += 2
                dve.wait_ge(place_step, chain)
                nc.vector.tensor_tensor(t["hot_tile"][:].rearrange("p t b i -> p (t b) i"), hot_f, flat(tokid),
                                        ALU.mult).then_inc(onehots_made, 1)
                nc.vector.tensor_tensor(t["hot_row"][:, :, 0], t["rowno"][:].unsqueeze(1).to_broadcast([P, TT, R]),
                                        t["jl"][:, :, 0].unsqueeze(2).to_broadcast([P, TT, R]),
                                        ALU.is_equal).then_inc(onehots_made, 1)
                for tt in range(TT):
                    nc.vector.tensor_tensor(t["hot_row"][:, tt, 1:], t["rowno"][:].unsqueeze(1).to_broadcast([P, B - 1, R]),
                                            t["jl"][:, tt, 1:].unsqueeze(2).to_broadcast([P, B - 1, R]),
                                            ALU.is_equal).then_inc(onehots_made, 1)
                    if tt == 0:
                        dve.wait_ge(perm_made, 1)
                        nc.vector.tensor_tensor(t["idx"][:R, 0], ST[0][:R, 0:NTALL], t["boff"][:R, 0],
                                                ALU.add).then_inc(idx_made, 1)

                def masks(b, par):
                    n = n_all[:, bass.ds(b, 1)]
                    j = t["jidx"][:, 0:NT]
                    at_least(dve, exp_done, 2 * NT * HEADS * (b - 1))
                    at_least(dve, out_done, NT * (b - 1))
                    nc.vector.tensor_scalar(t["valid"][:, par, :], j, n, None, ALU.is_lt).then_inc(mask_step, 1)
                    nc.vector.tensor_scalar(t["inv"][:, par, :], j, n, None, ALU.is_ge).then_inc(mask_step, 1)
                    nc.vector.tensor_scalar(t["kbias"][:, par, :], j, n, NEG, ALU.is_ge, ALU.mult).then_inc(mask_step, 1)
                    dve.wait_ge(mask_step, 3 * (b + 1))

                def zero_masked(b, par, k):
                    dve.wait_ge(gathered[k], 16 * (b + 1))
                    at_least(dve, xT_ready, NT * b + k + 1 - f.NA)
                    nc.vector.tensor_scalar(t["xv"][:R, k % f.NA, :], t["xg"][:R, par, k, :], t["valid"][:R, par, k:k + 1],
                                            None, ALU.mult).then_inc(xv_done, 1)

                def sum_tokens(b, par, k):
                    acc, r = t["xsum"], f.rows(k)
                    if k == 1:
                        for i in range(NT):
                            dve.wait_ge(gathered[i], 16 * (b + 1))
                        at_least(dve, gathered_tail, 16 * f.NTAIL * (b + 1))
                        at_least(dve, xbar_ready, b)
                        other = t["xg"][:R, par, 0, :]
                    else:
                        dve.wait_ge(xsum_step, (NTALL - 1) * b + k - 1)
                        other = acc[:r]
                    nc.vector.tensor_tensor(acc[:r], other, t["xg"][:r, par, k, :], ALU.add).then_inc(xsum_step, 1)

                def reduce_max(s, h, m):
                    dve.wait_ge(mx_ready, 2 * NT * s + m + 1)
                    nc.vector.tensor_reduce(t["mxp"][:R, h % 2, m // 2, m % 2:m % 2 + 1], MX[m % 2][:R, 0:H], AX.X,
                                            ALU.max).then_inc(mx_red, 1)
                    if m == 2 * NT - 1:
                        dve.wait_ge(mx_red, 2 * NT * (s + 1))
                        at_least(dve, mT_ready, s - 1)
                        nc.vector.tensor_reduce(t["mcol"][:R, h % 2, :], t["mxp"][:R, h % 2], AX.X, ALU.max,
                                                negate=True).then_inc(mcol_done, 1)

                def job(name, arg, bank, b, par, s):
                    if name == "mT":
                        h = arg
                        dve.wait_ge(mT_ready, s + 1)
                        at_least(dve, mrow_put[h % 2], 16 * ((HEADS // 2) * b + h // 2))
                        nc.vector.tensor_copy(t["mrow"][:, h % 2, :], MB[bank][:NT, 0:R]).then_inc(mrow_done, 1)
                    elif name == "proj":
                        g, half = arg
                        p = PAIRS * b + g
                        dve.wait_ge(hi_done, 2 * p + half + 1)
                        cols = slice(half * H, half * H + H)
                        q = t["Q"][:, g % 2, cols] if f.keeps_q else MB[bank][:, 0:H]
                        nc.vector.tensor_tensor(t["L"][:, g % 2, cols], q,
                                                t["H"][:, g % 2, cols].bitcast(F32), ALU.subtract).then_inc(lo_done, 1)
                    elif name == "out":
                        finish_tile(b - 1, 1 - par, arg, bank)
                    elif name == "xT":
                        if arg + 1 < NT:
                            zero_masked(b + 1, 1 - par, arg + 1)

                def reciprocal(s, quarter):
                    dve.wait_ge(rsum_done, s + 1)
                    cols = slice(H * quarter // 4, H * (quarter + 1) // 4)
                    nc.vector.reciprocal(t["rsum"][:, cols], t["rsum"][:, cols]).then_inc(recip_step, 1)

                def scale(s, h, b, par, half):
                    if half == 0:
                        dve.wait_ge(recip_step, 4 * (s + 1))
                        dve.wait_ge(ct_kept, s + 1)
                        if h == 0:
                            at_least(dve, out_ready, NT * (b - f.NC + 1))
                    r0, pr = DK * half, DK * (h % 2)
                    last = nc.vector.tensor_tensor(
                        t["ctxT"][pr:pr + DK, par % f.NC, h // 2, half * H:half * H + H],
                        t["rsum"][r0:r0 + DK, :], t["ctxraw"][r0:r0 + DK, :], ALU.mult)
                    if half == 1:
                        last.then_inc(ctx_done, 1)

                def alone(name, arg, b, par, h):
                    if name == "reciprocal":
                        reciprocal(HEADS * b + h, arg)
                    elif name == "scale":
                        if h < 0:
                            scale(HEADS * b + h, HEADS + h, b - 1, 1 - par, arg)
                        else:
                            scale(HEADS * b + h, h, b, par, arg)
                    elif name == "masks":
                        masks(b + 1, 1 - par)
                    elif name == "zero_masked":
                        zero_masked(b + 1, 1 - par, arg)
                    elif name == "sum_tokens":
                        sum_tokens(b + 1, 1 - par, arg)

                def finish_tile(b, par, k, bank):
                    xk = t["xg"][:R, par, k, :]
                    dve.wait_ge(out_ready, NT * b + k + 1)
                    dve.wait_ge(w_kept, b + 1)
                    at_least(dve, out_done, NT * b + k)
                    nc.vector.scalar_tensor_tensor(out=t["xsum"][:R], in0=MB[bank][:R, 0:D],
                                                   scalar=t["valid"][:R, par, k:k + 1], in1=xk, op0=ALU.mult,
                                                   op1=ALU.add).then_inc(out_step, 1)
                    dve.wait_ge(out_step, NT * b + k + 1)
                    nc.vector.scalar_tensor_tensor(out=xk, in0=t["w"][:R, par, :], scalar=t["inv"][:R, par, k:k + 1],
                                                   in1=t["xsum"][:R], op0=ALU.mult, op1=ALU.add).then_inc(out_done, 1)

                masks(0, 0)
                zero_masked(0, 0, 0)
                dve.wait_ge(perm_made, B)
                nc.vector.tensor_tensor(t["idx"][:R, 1:],
                                        ST[2][:R, NTALL:B * NTALL].rearrange("p (b i) -> p b i", b=B - 1),
                                        t["boff"][:R, 1:], ALU.add).then_inc(idx_made, 1)
                quarter = -(-(NTALL - 1) // 4)
                for name, arg, bank, before in plan[0]:
                    if name == "mT":
                        for m in range(2 * NT):
                            reduce_max(0, 0, m)
                    job(name, arg, bank, -1 if name == "xT" else 0, 1 if name == "xT" else 0, 0)
                    if name == "mT":
                        for m in range(2 * NT):
                            reduce_max(1, 1, m)
                    if name == "proj" and arg[0] < 2:
                        first = 1 + (2 * arg[0] + arg[1]) * quarter
                        for k in range(first, min(first + quarter, NTALL)):
                            sum_tokens(0, 0, k)

                def batch(b, par, table, has_prev, has_next):
                    extras = vector_jobs(f, has_prev, has_next)
                    late = []
                    for h in range(HEADS):
                        s = HEADS * b + h
                        for k in range(NT):
                            for a in range(2):
                                if h < HEADS - 2 or has_next:
                                    reduce_max(s + 2, h + 2, 2 * k + a)
                                due = [j for j in table[h, k] if j[0] not in LATE] if a == 1 else late
                                for name, arg, bank, before in due:
                                    job(name, arg, bank, b, par, s + 1 if name == "mT" else s - 1)
                                if a == 1:
                                    late = [j for j in table[h, k] if j[0] in LATE]
                                for name, arg in extras[h, k, a]:
                                    alone(name, arg, b, par, h - 1 if k > 0 else h - 2)
                    assert not late

                def tail(jobs):
                    if f.late_scale:
                        alone("scale", 1, B, B % 2, -2)
                    for name, arg, bank, before in jobs:
                        job(name, arg, bank, B, B % 2, HEADS * B - 1)
                        if name == "L":
                            for quarter in range(4):
                                alone("reciprocal", quarter, B, B % 2, -1)
                            for half in range(2):
                                alone("scale", half, B, B % 2, -1)

                run_batches(dve, f, plan, batch, tail)

            fitting_form(dve, body)

        @block.tensor
        def _(pe):
            pe.wait_ge(consts_made, 8)
            pe.wait_ge(mask_cast, 1)
            for tt in range(TT):
                for u in range(tt + 1):
                    nc.tensor.matmul(ST[0][:, B * tt:B * tt + B], tri[:] if u == tt else ones_b[:], mask_b[:, u, :],
                                     start=(u == 0), stop=(u == tt))
            for u in range(TT):
                last = nc.tensor.matmul(ST[1][:, 0:B], ones_b[:], mask_b[:, u, :], start=(u == 0), stop=(u == TT - 1))
            last.then_inc(counted, 1)

            def body(f, t, plan):
                NT, R, C, H, NTALL = f.NT, f.R, f.C, f.H, f.NTALL

                def order(b, bank, col):
                    for tt in range(TT):
                        last = nc.tensor.matmul(bank[:R, col], t["hot_row"][:, tt, b, :], t["hot_tile"][:, tt, b, :],
                                                start=(tt == 0), stop=(tt == TT - 1))
                    last.then_inc(perm_made, 1)

                pe.wait_ge(onehots_made, 2)
                order(0, ST[0], slice(0, NTALL))
                pe.wait_ge(loaded, 48)
                for k in range(KD):
                    at_least(pe, g_kept, k - 1)
                    for m in range(KD):
                        last = nc.tensor.matmul(MB[k % 2][:, 0:D], wq_sb[:, m, P * k:P * k + P], woT_sb[:, m, :],
                                                start=(m == 0), stop=(m == KD - 1))
                    last.then_inc(g_made, 1)

                pe.wait_ge(onehots_made, TT + 2)
                group = next(n for n in (5, 3, 2, 1) if (B - 1) % n == 0)
                with pe.Fori(0, (B - 1) // group) as g:
                    for i in range(1, group + 1):
                        order(g * group + i, ST[2], bass.ds((g * group + i) * NTALL, NTALL))
                pe.wait_ge(g_kept, KD)

                def tile_cols(i):
                    return slice(R * i, R * i + R)

                def half_cols(i):
                    return slice(H * i, H * i + H)

                def max_scores(s, s4, h, m):
                    ops = t["ops"][:, h % SLOTS]
                    if m == 0:
                        pe.wait_ge(dup[h % SLOTS], 96 * (s4 + 1))
                    at_least(pe, mx_red, 2 * NT * s + m - 1)
                    nc.tensor.matmul(MX[m % 2][:R, 0:H], ops[:, OPA, tile_cols(m // 2)], ops[:, OPB, half_cols(m % 2)],
                                     start=True, stop=True).then_inc(mx_ready, 1)

                def scores(s, s2, h, k):
                    ops = t["ops"][:, h % SLOTS]
                    if k == 0:
                        pe.wait_ge(mrow_put[h % 2], 16 * (s2 + 1))
                    banks, count = [], 2 * NT * HEADS
                    for half in range(2):
                        u = 2 * (NT * h + k) + half
                        banks.append(ST[u % 3])
                        last_user = u - 3 if u >= 3 else next(v for v in range(-1, -4, -1) if (count + v - u) % 3 == 0)
                        at_least(pe, exp_done, 2 * NT * (s - h) + last_user + 1)
                        nc.tensor.matmul(banks[half][:R, 0:H], ops[:, OPA, tile_cols(k)], ops[:, OPB, half_cols(half)],
                                         start=True, stop=False)
                    for half in range(2):
                        nc.tensor.matmul(banks[half][:R, 0:H], ops[:, OPY, tile_cols(k)], ops[:, OPX, half_cols(half)],
                                         start=False, stop=True).then_inc(s_ready, 1)

                def times_values(s, p, h, k):
                    if k == 0:
                        at_least(pe, ct_kept, s)
                        at_least(pe, v_kept, 2 * p + 2)
                    for half in range(2):
                        pe.wait_ge(exp_done, 2 * (NT * s + k) + half + 1)
                        last = nc.tensor.matmul(CT[DK * half:DK * half + DK, 0:H],
                                                t["V"][:R, (h // 2) % 2, k, DK * (h % 2):DK * (h % 2) + DK],
                                                t["Pt"][:R, (NT * h + k) % f.NP, half, :],
                                                start=(k == 0), stop=(k == NT - 1))
                    last.then_inc(pv_done, 1)

                def bank_left(name, arg, b):
                    if name == "xT":
                        at_least(pe, xT_kept, NT * (b + 1) + arg + 1)
                    elif name == "xbar":
                        at_least(pe, xbar_kept, b + 2)
                    elif name == "w":
                        at_least(pe, w_kept, b + 2)
                    elif name == "proj":
                        at_least(pe, q_kept if f.keeps_q else lo_done, 2 * (PAIRS * b + arg[0]) + arg[1] + 1)
                    elif name == "V":
                        at_least(pe, v_kept, 2 * (PAIRS * b + arg[0]) + arg[1] + 1)
                    elif name == "mT":
                        at_least(pe, mrow_done, HEADS * b + arg + 1)
                    elif name == "L":
                        at_least(pe, rsum_done, HEADS * b + arg + 1)
                    elif name == "out":
                        at_least(pe, out_step, NT * (b - 1) + arg + 1)

                def job(name, arg, bank, before, b, par, s, chunks=range(KD)):
                    mb = MB[bank]
                    if before and chunks[0] == 0:
                        bank_left(before[0], before[1], b + before[2])
                    if name == "xT":
                        pe.wait_ge(xv_done, NT * (b + 1) + arg + 1)
                        for c in range(KD):
                            last = nc.tensor.transpose(mb[:, R * c:R * c + R], t["xv"][:R, arg % f.NA, P * c:P * c + P],
                                                       ident[:R, :R])
                        last.then_inc(xT_ready, 1)
                    elif name == "xbar":
                        pe.wait_ge(xsum_step, (NTALL - 1) * (b + 2))
                        for c in range(KD):
                            last = nc.tensor.matmul(mb[:, P * c:P * c + P], t["xsum"][:R, P * c:P * c + P], meanT[:R, :],
                                                    start=True, stop=True)
                        last.then_inc(xbar_ready, 1)
                    elif name == "w":
                        if chunks[0] == 0:
                            pe.wait_ge(xbar_kept, b + 2)
                        for c in chunks:
                            last = nc.tensor.matmul(mb[:, 0:D], t["xbarT"][:, c, :], G[:, c, :],
                                                    start=(c == 0), stop=(c == KD - 1))
                        if c == KD - 1:
                            last.then_inc(w_ready, 1)
                    elif name == "proj":
                        g, half = arg
                        if chunks[0] == 0:
                            pe.wait_ge(xT_kept, NT * (b + g // PAIRS + 1))
                        for c in chunks:
                            last = nc.tensor.matmul(mb[:, 0:H], wqT_sb[:, c, P * (g % PAIRS):P * (g % PAIRS) + P],
                                                    t["xcT"][:, c, half_cols(half)], start=(c == 0), stop=(c == KD - 1))
                        if c == KD - 1:
                            last.then_inc(proj_ready, 1)
                    elif name == "V":
                        g, part = arg
                        pe.wait_ge(q_kept if f.keeps_q else lo_done, 2 * (PAIRS * b + g) + 2)
                        for i in range(min(4, NT - 4 * part)):
                            cols = tile_cols(4 * part + i)
                            if f.keeps_q:
                                last = nc.tensor.transpose(mb[:R, P * i:P * i + P], t["Q"][:, g % 2, cols], ident[:])
                                continue
                            nc.tensor.matmul(mb[:R, P * i:P * i + P], t["H"][:, g % 2, cols], identR[:],
                                             start=True, stop=False)
                            last = nc.tensor.matmul(mb[:R, P * i:P * i + P], t["L"][:, g % 2, cols], identR[:],
                                                    start=False, stop=True)
                        last.then_inc(v_ready, 1)
                    elif name == "mT":
                        pe.wait_ge(mcol_done, s + 1)
                        nc.tensor.transpose(mb[:NT, 0:R], t["mcol"][:R, arg % 2, :], ident[:R, :R]).then_inc(mT_ready, 1)
                    elif name == "L":
                        pe.wait_ge(pacc_step, (NT - 1) * (s + 1))
                        for half in range(2):
                            last = nc.tensor.matmul(mb[DK * half:DK * half + DK, 0:H], ones64[:R, :],
                                                    t["Pacc"][:R, arg % HEADS % f.NA, half, :], start=True, stop=True)
                        last.then_inc(l_ready, 1)
                    elif name == "out":
                        if chunks[0] == 0:
                            pe.wait_ge(ctx_done, HEADS * b)
                        for c in chunks:
                            last = nc.tensor.matmul(mb[:R, 0:D], t["ctxT"][:, (1 - par) % f.NC, c, tile_cols(arg)],
                                                    woT_sb[:, c, :], start=(c == 0), stop=(c == KD - 1))
                        if c == KD - 1:
                            last.then_inc(out_ready, 1)

                for (name, arg, bank, before), (_, _, b) in zip(plan[0], front_jobs(f)):
                    if before:
                        bank_left(*before)
                    if name == "mT":
                        for m in range(2 * NT):
                            max_scores(0, 0, 0, m)
                    if name == "xbar":
                        for m in range(2 * NT):
                            max_scores(1, 0, 1, m)
                    job(name, arg, bank, None, b, b % 2, 0)

                def misc(jobs, b, par, s, part):
                    for name, arg, bank, before in jobs:
                        sj = s + 1 if name == "mT" else s - 1
                        if name in TWO_PARTS:
                            job(name, arg, bank, before, b, par, sj, range(KD // 2 * part, KD // 2 * (part + 1)))
                        elif part == (name in ("xT", "mT")):
                            job(name, arg, bank, before, b, par, sj)

                def batch(b, par, table, has_prev, has_next):
                    for h in range(HEADS):
                        s = HEADS * b + h
                        for k in range(NT):
                            ahead = h < HEADS - 2 or has_next
                            if ahead:
                                max_scores(s + 2, 2 * b + (h + 2) // SLOTS, h + 2, 2 * k)
                            scores(s, (HEADS // 2) * b + h // 2, h, k)
                            misc(table[h, k], b, par, s, 0)
                            if ahead:
                                max_scores(s + 2, 2 * b + (h + 2) // SLOTS, h + 2, 2 * k + 1)
                            if k > 0:
                                times_values(s, PAIRS * b + h // 2, h, k - 1)
                            elif h > 0:
                                times_values(s - 1, PAIRS * b + (h - 1) // 2, h - 1, NT - 1)
                            elif has_prev:
                                times_values(s - 1, PAIRS * b - 1, HEADS - 1, NT - 1)
                            misc(table[h, k], b, par, s, 1)

                def tail(jobs):
                    times_values(HEADS * B - 1, PAIRS * B - 1, HEADS - 1, NT - 1)
                    for name, arg, bank, before in jobs:
                        job(name, arg, bank, before, B, B % 2, HEADS * B - 1)

                run_batches(pe, f, plan, batch, tail)

            fitting_form(pe, body)


def kernel(x, cond_2048, L0_cond_Wq, L0_cond_Wo):
    import numpy as np
    import concourse.bacc as bacc
    from concourse.bass_utils import run_bass_kernel_spmd

    x = np.asarray(x)
    B, D, T = x.shape
    mask = np.asarray(cond_2048)
    wq, wo = np.asarray(L0_cond_Wq), np.asarray(L0_cond_Wo)
    arrays = {
        "x_rows": np.ascontiguousarray(x.transpose(0, 2, 1)).reshape(B * T, D),
        "mask_t": np.ascontiguousarray(mask.reshape(B, T // P, P).transpose(2, 1, 0)).reshape(P, -1),
        "wq": np.ascontiguousarray(wq),
        "wqT": np.ascontiguousarray(wq.T),
        "woT": np.ascontiguousarray(wo.T),
    }
    nc = bacc.Bacc("TRN2", target_bir_lowering=False, num_devices=1)
    ins = [nc.dram_tensor(n, a.shape, F32, kind="ExternalInput").ap() for n, a in arrays.items()]
    out = nc.dram_tensor("out_rows", (B * T, D), F32, kind="ExternalOutput").ap()
    attention_kernel(nc, *ins, out, B, T, D)
    got = run_bass_kernel_spmd(nc, [arrays], core_ids=[0]).results[0]["out_rows"]
    return np.ascontiguousarray(got.reshape(B, T, D).transpose(0, 2, 1))
```

```python
from contextlib import ExitStack

import concourse.bass as bass
from concourse import mybir

P = 128
F32 = mybir.dt.float32
F32R = mybir.dt.float32r
BF16 = mybir.dt.bfloat16
F16 = mybir.dt.float16
I32 = mybir.dt.int32
ALU = mybir.AluOpType
ACT = mybir.ActivationFunctionType
AX = mybir.AxisListType

HEADS = 8
DK = 64
PAIRS = HEADS // 2
NEG = -1e30
SLOTS = 4
OPA, OPB, OPY, OPX = range(4)


PROJ_AT = [(0, 3), (1, 3), (2, 3), (4, 2), (4, 3), (5, 3), (6, 3), (7, 3)]
V_AT = (0, 1)
XT_AT = [(3, 1), (3, 2), (3, 3), (3, 4), (4, 0)]
OUT_AT = [(1, 2), (1, 4), (2, 0), (2, 2), (2, 3)]
XBAR_AT, W_AT = (7, 1), (7, 3)
RECIPROCAL_AT = [(2, 1), (2, 1), (3, 0), (3, 1)]
SCALE_AT = [(4, 1), (0, 0)]
CTX_LOW_AT = (2, 0)
MASKS_AT, MASKED_AT = (2, 4, 1), (3, 0)
SUM_AT = [(4, 0, 1), (4, 1, 0), (4, 1, 1), (5, 1, 0), (5, 1, 1), (5, 2, 1), (6, 1, 0), (6, 1, 1), (6, 2, 0)]
ADD_W_FROM, SCATTER_TAIL_FROM, GATHER_TAIL_FROM = 0, 5, 17


class Form:

    def __init__(self, name, NT, R, T, NP, NA, split):
        self.name, self.NT, self.R, self.T = name, NT, R, T
        self.C = NT * R
        self.H = self.C // 2
        self.NTALL = -(-T // R)
        self.RL = T - R * (self.NTALL - 1)
        self.NTAIL = self.NTALL - NT
        self.NP, self.NA = NP, NA
        self.split = split

    def rows(self, k):
        return self.RL if k == self.NTALL - 1 else self.R


def misc_jobs(form, has_prev, has_next):
    NT = form.NT
    table = {(h, k): [] for h in range(HEADS) for k in range(NT)}
    steps = list(table)
    for h in range(HEADS):
        if h % 2 == 1 and (h < 7 or has_next):
            table[h, V_AT[0]].append(("V", ((h + 1) // 2, 0)))
            table[h, V_AT[1]].append(("V", ((h + 1) // 2, 1)))
        if h > 0 or has_prev:
            table[h, 2].append(("L", h - 1))
    if has_prev:
        for k, at in enumerate(out_steps(form)):
            table[at].append(("out", k))
    for at, pair in zip(PROJ_AT, ((2, 1), (3, 0), (3, 1), (4, 0), (4, 1), (5, 0), (5, 1), (6, 0))):
        if at < (4, 0) or has_next:
            table[at].append(("proj", pair))
    if has_next:
        for k in range(NT):
            table[XT_AT[k] if form.split else (3, k)].append(("xT", k))
        table[XBAR_AT].append(("xbar", 0))
        table[W_AT].append(("w", 0))
    for h in range(HEADS - 1 + has_next):
        table[h, 0].append(("mT", h + 1))
    for jobs in table.values():
        assert all(name not in TWO_PARTS for name, _ in jobs[:-2])
    return table


TWO_PARTS = ("proj", "out", "w")
LATE = ("proj", "out", "w", "xT")


def out_steps(form):
    return OUT_AT if form.NT == 5 else \
        [(0, 5), (0, 5), (0, 6), (0, 6), (0, 7), (0, 7), (1, 1), (1, 3)]


def pool_jobs(form, has_prev, has_next):
    NT, NTAIL = form.NT, form.NTAIL
    table = {(h, k): [] for h in range(HEADS) for k in range(NT)}
    steps = list(table)
    scatters = [steps[steps.index(at) + (1 if form.split else 2)] for at in out_steps(form)]
    gathers = [max(steps[steps.index(at) + 2], (1, 4)) for at in scatters]
    for i in range(NTAIL):
        table[steps[ADD_W_FROM + i]].append(("add_w", i))
        table[steps[SCATTER_TAIL_FROM + i]].append(("scatter_tail", i))
    if has_prev:
        for i, at in enumerate(scatters):
            table[at].append(("scatter", i))
    if has_next:
        for i in range(NTAIL):
            table[steps[GATHER_TAIL_FROM + i]].append(("gather", NT + i))
        for i in range(NT):
            table[gathers[i]].append(("gather", i))
    return table


def masked_from(form):
    return MASKED_AT if form.split else (2, 4)


def vector_jobs(form, has_prev, has_next):
    table = {(h, k, a): [] for h in range(HEADS) for k in range(form.NT) for a in range(2)}
    for h in range(HEADS):
        if h > 0 or has_prev:
            for quarter, at in enumerate(RECIPROCAL_AT if form.split else [(2, 1), (3, 0), (3, 1), (4, 0)]):
                table[(h, *at)].append(("reciprocal", quarter))
            table[(h, *SCALE_AT[0]) if form.split else (h, 4, 1)].append(("scale", 0))
            if not form.split:
                table[h, 4, 1].append(("scale", 1))
        if form.split and (h > 1 or has_prev):
            table[(h, *SCALE_AT[1])].append(("scale", 1))
            if h % 2:
                table[(h, *CTX_LOW_AT)].append(("ctx_low", 0))
    if has_next:
        table[MASKS_AT if form.split else (2, 3, 1)].append(("masks", 0))
        steps = SUM_AT
        for i in range(1, form.NTALL):
            table[steps[i - 1]].append(("sum_tokens", i))
    return table


def front_jobs(form):
    return ([("xT", k, -1) for k in range(form.NT)] + [("proj", (0, 0), 0), ("proj", (0, 1), 0)]
            + [("V", (0, 0), 0), ("V", (0, 1), 0), ("proj", (1, 0), 0), ("proj", (1, 1), 0)]
            + [("proj", (2, 0), 0), ("mT", 0, 0), ("xbar", 0, -1), ("w", 0, -1)])


def tail_jobs(form):
    return [("L", -1, 0)] + [("out", k, 0) for k in range(form.NT)]


def with_banks(form):
    def give(jobs, start, two_back):
        out = []
        for i, (name, arg, back) in enumerate(jobs):
            out.append((name, arg, (start + i) % 2, two_back[-2]))
            two_back = [two_back[-1], (name, arg, back)]
        return out, two_back

    def give_table(table, start, two_back):
        steps = list(table)
        flat, two_back = give([(*job, 0) for at in steps for job in table[at]], start, two_back)
        flat = iter(flat)
        return {at: [next(flat) for _ in table[at]] for at in steps}, two_back

    def one_later(two_back):
        return [(name, arg, back - 1) for name, arg, back in two_back]

    def count(table):
        return sum(map(len, table.values()))

    tables = [misc_jobs(form, False, True), misc_jobs(form, True, True), misc_jobs(form, True, False)]
    assert count(tables[1]) % 2 == 0
    front, end = give(front_jobs(form), 0, [None, None])
    at = len(front)
    first, end = give_table(tables[0], at, end)
    at += count(tables[0])
    mid, same_end = give_table(tables[1], at, one_later(end))
    assert same_end == end
    last, end = give_table(tables[2], at, one_later(end))
    tail, _ = give(tail_jobs(form), at + count(tables[2]), one_later(end))
    return front, first, mid, last, tail


def at_least(eng, sem, value):
    if not isinstance(value, int) or value > 0:
        eng.wait_ge(sem, value)


def wait_alone(eng, sem, value, passed):
    if not isinstance(value, int) or value > 0:
        eng.wait_ge(sem, value)
        eng.sem_inc(passed, 1)


def attention_kernel(nc, x_rows, mask_t, wq, wqT, woT, out_rows, B, T, D):
    KD = D // P
    TT = T // P
    forms = [Form("small", 5, 108, T, 4, 2, True), Form("middle", 5, 116, T, 4, 2, True),
             Form("full", 8, 128, T, 2, 1, False)]
    SCALE = float(DK) ** -0.5

    with ExitStack() as ctx:
        def sb(name, shape, dt, stack=ctx):
            return stack.enter_context(nc.sbuf_tensor(name, shape, dt))

        def psum(name, shape, dt):
            return ctx.enter_context(nc.psum_tensor(name, shape, dt))

        def sem(name):
            return ctx.enter_context(nc.semaphore(name))

        ST = [psum(f"scores{i}", [P, 512], F32) for i in range(3)]
        MX = [psum(f"max_scores{i}", [P, 512], F32) for i in range(2)]
        CT = psum("ctx_psum", [P, 512], F32)
        MB = [psum(f"misc{i}", [P, 512], F32) for i in range(2)]

        G = sb("G", [P, KD, D], F32)
        ident = sb("ident", [P, P], F32)
        identR = sb("identR", [P, P], F32R)
        ones64 = sb("ones64", [P, DK], F32)
        tiny = sb("tiny", [P, 1], F32)
        meanT = sb("meanT", [P, P], F32)
        n_all = sb("n_all", [P, B], F32)
        n_max = sb("n_max", [P, 1], F32)
        n_max_i = sb("n_max_i", [P, 1], I32)
        pos = sb("pos", [P, TT, B], F32)
        tokid = sb("tokid", [P, TT, B], F32)

        sems = {n: sem(n) for n in (
            "loaded mask_loaded consts_made iotas_made consts_cast mask_cast counted pos_step pos_done g_made g_kept "
            "place_step onehots_made perm_made idx_made jidx_made ops_cleared").split()}
        loaded, mask_loaded, consts_made, iotas_made, consts_cast, mask_cast, counted, pos_step, pos_done, g_made, \
            g_kept, place_step, onehots_made, perm_made, idx_made, jidx_made, ops_cleared = sems.values()
        s_ready, mx_ready, pv_done = sem("s_ready"), sem("mx_ready"), sem("pv_done")
        xT_ready, xbar_ready, w_ready = sem("xT_ready"), sem("xbar_ready"), sem("w_ready")
        proj_ready, v_ready, mT_ready = sem("proj_ready"), sem("v_ready"), sem("mT_ready")
        l_ready, out_ready = sem("l_ready"), sem("out_ready")
        exp_done, xT_kept, hi_done, v_kept = sem("exp_done"), sem("xT_kept"), sem("hi_done"), sem("v_kept")
        xbar_kept, w_kept, ct_kept, q_kept = sem("xbar_kept"), sem("w_kept"), sem("ct_kept"), sem("q_kept")
        whi_done, ctx_hi_done = sem("whi_done"), sem("ctx_hi_done")
        mx_red, mcol_done, mrow_done, lo_done = sem("mx_red"), sem("mcol_done"), sem("mrow_done"), sem("lo_done")
        ctx_done, xv_done, xsum_step, mask_step = sem("ctx_done"), sem("xv_done"), sem("xsum_step"), sem("mask_step")
        out_step, out_done, rsum_done = sem("out_step"), sem("out_done"), sem("rsum_done")
        recip_step, xlo_done, ctx_lo_done = sem("recip_step"), sem("xlo_done"), sem("ctx_lo_done")
        wlo_done = sem("wlo_done")
        pacc_step, idx_copied, tail_added = sem("pacc_step"), sem("idx_copied"), sem("tail_added")
        sp_passed, pool_passed = sem("sp_passed"), sem("pool_passed")
        dup = [sem(f"dup{i}") for i in range(SLOTS)]
        mrow_put = [sem(f"mrow_put{i}") for i in range(2)]
        gathered = [sem(f"gathered{i}") for i in range(TT)]
        scattered = [sem(f"scattered{i}") for i in range(TT)]
        gathered_tail = sem("gathered_tail")
        scattered_tail = [sem(f"scattered_tail{i}") for i in range(2)]

        start = ExitStack()
        mask_f = sb("mask_f", [P, TT, B], F32, start)
        mask_b = sb("mask_b", [P, TT, B], BF16, start)
        tri = sb("tri", [P, P], BF16, start)
        ones_b = sb("ones_b", [P, P], BF16, start)
        cnt = sb("cnt", [P, TT, B], F32, start)
        behind = sb("behind", [P, TT, B], F32, start)
        tokid_i = sb("tokid_i", [P, TT, B], I32, start)
        start.close()

        tensors = [{} for _ in forms]
        for f, t in zip(forms, tensors):
            own = ExitStack()

            def keep(name, shape, dt, stack=own, t=t, f=f):
                t[name] = sb(f"{f.name}_{name}", shape, dt, stack)

            keep("xg", [P, 2, f.NTALL, D], F32)
            keep("xcT", [P, KD, f.C], F32R if f.split else F32)
            keep("idx", [P, B, f.NTALL], I32)
            keep("jidx", [P, f.NTALL], F32)
            keep("idx_cur", [P, 2, f.NTALL], I32)
            keep("valid", [P, 2, f.NT], F32)
            keep("inv", [P, 2, f.NT], F32)
            keep("kbias", [P, 2, f.NT], F32)
            tables = ExitStack()
            t["jh"] = sb(f"{f.name}_jh", [P, TT, B], F32, tables)
            t["jl"] = sb(f"{f.name}_jl", [P, TT, B], F32, tables)
            t["tileno"] = sb(f"{f.name}_tileno", [P, f.NTALL], F32, tables)
            t["tileno_i"] = sb(f"{f.name}_tileno_i", [P, f.NTALL], I32, tables)
            t["rowno"] = sb(f"{f.name}_rowno", [P, f.R], F32, tables)
            t["rowno_i"] = sb(f"{f.name}_rowno_i", [P, f.R], I32, tables)
            t["jidx_i"] = sb(f"{f.name}_jidx_i", [P, f.NTALL], I32, tables)
            t["boff_i"] = sb(f"{f.name}_boff_i", [P, B, f.NTALL], I32, tables)
            t["boff"] = sb(f"{f.name}_boff", [P, B, f.NTALL], F32, tables)
            t["hot_tile_f"] = sb(f"{f.name}_hot_tile_f", [P, TT, B, f.NTALL], F32, tables)
            t["hot_tile"] = sb(f"{f.name}_hot_tile", [P, TT, B, f.NTALL], F16, tables)
            t["hot_row"] = sb(f"{f.name}_hot_row", [P, TT, B, f.R], F16, tables)
            tables.close()
            keep("ops", [P, SLOTS, 4, f.C], F32R)
            keep("H", [P, 2, f.C], F32R)
            keep("L", [P, 2, f.C], F32R)
            if f.split:
                keep("Q", [P, 2, f.C], F32)
            keep("V", [P, 2, f.NT, P], F32)
            keep("Pt", [P, f.NP, 2, f.H], F32)
            keep("Pacc", [P, f.NA, 2, f.H], F32)
            keep("ctxraw", [P, f.H], F32)
            keep("rsum", [P, f.H], F32)
            keep("w", [P, 2, D], F32)
            keep("xbarT", [P, KD, P], F32)
            keep("xsum", [P, D], F32)
            keep("xv", [P, f.NA, D], F32)
            keep("mxp", [P, 2, f.NT, 2], F32)
            keep("mcol", [P, 2, f.NT], F32)
            keep("mrow", [f.NT, 2, f.R], F32R)
            if f.split:
                for name in ("wqT_hi", "wqT_lo", "woT_hi", "woT_lo"):
                    keep(name, [P, KD, D], F32R)
                keep("xcT_lo", [P, KD, f.C], F32R)
                keep("ctx", [P, 2, f.C], F32)
                keep("ctxT", [P, KD, f.C], F32R)
                keep("ctxT_lo", [P, KD, f.C], F32R)
            else:
                over = ExitStack()
                sb("under_wq", [P, KD, f.C - D], F32, over)
                wq_sb = sb("wq_sb", [P, KD, D], F32, over)
                over.close()
                keep("ctxT", [P, KD, f.C], F32)
                wqT_sb = sb("wqT_sb", [P, KD, D], F32, own)
                woT_sb = sb("woT_sb", [P, KD, D], F32, own)
            own.close()

        block = ctx.enter_context(nc.Block())
        plans = [with_banks(f) for f in forms]

        def run_batches(eng, form, plan, batch, tail):
            front, first, mid, last, tail_plan = plan
            batch(0, 0, first, False, True)
            batch(1, 1, mid, True, True)
            with eng.Fori(2, B - 2, 2) as b:
                batch(b, 0, mid, True, True)
                batch(b + 1, 1, mid, True, True)
            batch(B - 2, 0, mid, True, True)
            batch(B - 1, 1, last, True, False)
            tail(tail_plan)

        def fitting_form(eng, body):
            eng.wait_ge(pos_done, 2)
            n = eng.value_load(n_max_i[0:1, 0:1], min_val=0, max_val=T)
            with eng.If(n <= forms[0].C):
                body(forms[0], tensors[0], plans[0])
            with eng.Else():
                with eng.If(n <= forms[1].C):
                    body(forms[1], tensors[1], plans[1])
                with eng.Else():
                    body(forms[2], tensors[2], plans[2])

        @block.sync
        def _(sp):
            sp.dma_start(mask_f[:].rearrange("p t b -> p (t b)"), mask_t).then_inc(mask_loaded, 16)
            for dst, src in ((wq_sb, wq), (woT_sb, woT), (wqT_sb, wqT)):
                sp.dma_start(dst[:], src.rearrange("(k p) n -> p k n", p=P)).then_inc(loaded, 16)

            def body(f, t, plan):
                NT, R = f.NT, f.R

                def copy_operands(s, h):
                    slot, r0, stage = h % SLOTS, DK * (h % 2), (h // 2) % 2
                    hi = t["H"][r0:r0 + DK, stage, :]
                    lo = t["L"][r0:r0 + DK, stage, :]
                    wait_alone(sp, lo_done, s - h % 2 + 2, sp_passed)
                    wait_alone(sp, s_ready, 2 * NT * (s - SLOTS + 1), sp_passed)
                    for op, half, src in ((OPA, 0, hi), (OPA, 1, lo), (OPB, 0, hi), (OPB, 1, hi), (OPY, 0, hi),
                                          (OPX, 0, lo)):
                        sp.dma_start(t["ops"][DK * half:DK * half + DK, slot, op, :].bitcast(F32),
                                     src.bitcast(F32)).then_inc(dup[slot], 16)

                def put_max_row(s, h):
                    wait_alone(sp, mrow_done, s + 1, sp_passed)
                    sp.dma_start(t["ops"][DK:DK + 1, h % SLOTS, OPX, :].bitcast(F32).rearrange("o (k r) -> o k r", r=R),
                                 t["mrow"][:, h % 2, :].bitcast(F32)).then_inc(mrow_put[h % 2], 16)

                sp.wait_ge(ops_cleared, 3)
                copy_operands(0, 0)
                copy_operands(1, 1)
                copy_operands(2, 2)
                put_max_row(0, 0)

                def batch(b, par, table, has_prev, has_next):
                    for h in range(HEADS):
                        s = HEADS * b + h
                        if h < HEADS - 1 or has_next:
                            put_max_row(s + 1, h + 1)
                        if h < HEADS - 3 or has_next:
                            copy_operands(s + 3, h + 3)

                run_batches(sp, f, plan, batch, lambda tail: None)

            fitting_form(sp, body)

        @block.gpsimd
        def _(pool):
            nc.gpsimd.memset(ident[:], 0.0).then_inc(consts_made, 1)
            nc.gpsimd.memset(tri[:], 1.0).then_inc(consts_made, 1)
            nc.gpsimd.memset(ones_b[:], 1.0).then_inc(consts_made, 1)
            nc.gpsimd.memset(ones64[:], 1.0).then_inc(consts_made, 1)
            nc.gpsimd.memset(meanT[:], 1.0 / T).then_inc(consts_made, 1)
            nc.gpsimd.memset(tiny[:], 1e-30).then_inc(consts_made, 1)
            pool.wait_ge(consts_made, 6)
            nc.gpsimd.affine_select(out=ident[:], in_=ident[:], compare_op=ALU.not_equal, fill=1.0, base=0,
                                    pattern=[[-1, P]], channel_multiplier=1).then_inc(consts_made, 1)
            nc.gpsimd.affine_select(out=tri[:], in_=tri[:], compare_op=ALU.is_ge, fill=0.0, base=0,
                                    pattern=[[1, P]], channel_multiplier=-1).then_inc(consts_made, 1)
            nc.gpsimd.iota(tokid_i[:], pattern=[[P, TT], [0, B]], base=0, channel_multiplier=1).then_inc(iotas_made, 1)

            def body(f, t, plan):
                NT, R, NTALL, NTAIL = f.NT, f.R, f.NTALL, f.NTAIL
                nc.gpsimd.iota(t["tileno_i"][:], pattern=[[1, NTALL]], base=0, channel_multiplier=0).then_inc(iotas_made, 1)
                nc.gpsimd.iota(t["rowno_i"][:], pattern=[[1, R]], base=0, channel_multiplier=0).then_inc(iotas_made, 1)
                nc.gpsimd.iota(t["jidx_i"][:], pattern=[[R, NTALL]], base=0, channel_multiplier=1).then_inc(iotas_made, 1)
                nc.gpsimd.iota(t["boff_i"][:], pattern=[[T, B], [0, NTALL]], base=0, channel_multiplier=0).then_inc(iotas_made, 1)
                def copy_order(b, par, k):
                    copies = NT + (1 if NTAIL else 0)
                    if k == NT:
                        at_least(pool, scattered_tail[par], 8 * NTAIL * (b - par))
                        nc.gpsimd.tensor_copy(t["idx_cur"][:R, par, NT:], t["idx"][:R, b, NT:]).then_inc(idx_copied, 1)
                        wait_alone(pool, idx_copied, copies * b + NT + 1, pool_passed)
                    if k < NT:
                        at_least(pool, scattered[k], 16 * (b - 1))
                        nc.gpsimd.tensor_copy(t["idx_cur"][:R, par, k:k + 1],
                                              t["idx"][:R, b, k:k + 1]).then_inc(idx_copied, 1)
                        wait_alone(pool, idx_copied, copies * b + k + 1, pool_passed)

                def gather(b, par, k):
                    r = f.rows(k)
                    nc.gpsimd.indirect_dma_start(
                        out=t["xg"][:r, par, k, :], out_offset=None, in_=x_rows,
                        in_offset=bass.IndirectOffsetOnAxis(ap=t["idx_cur"][:r, par, k:k + 1], axis=0),
                    ).then_inc(gathered[k] if k < NT else gathered_tail, 16)

                def scatter(par, k, done):
                    r = f.rows(k)
                    nc.gpsimd.indirect_dma_start(
                        out=out_rows, in_=t["xg"][:r, par, k, :], in_offset=None,
                        out_offset=bass.IndirectOffsetOnAxis(ap=t["idx_cur"][:r, par, k:k + 1], axis=0),
                    ).then_inc(done, 16)

                def add_w(b, par, i):
                    if i == 0:
                        at_least(pool, w_kept, b + 1)
                        at_least(pool, xsum_step, (NTALL - 1) * (b + 1))
                    r, xk = f.rows(NT + i), t["xg"][:, par, NT + i, :]
                    nc.gpsimd.tensor_tensor(xk[:r], xk[:r], t["w"][:r, par, :], ALU.add).then_inc(tail_added, 1)

                def scatter_tail(b, par, i):
                    if i == 0:
                        wait_alone(pool, tail_added, NTAIL * (b + 1), pool_passed)
                    scatter(par, NT + i, scattered_tail[par])

                def job(name, arg, b, par):
                    if name == "scatter":
                        wait_alone(pool, out_done, NT * (b - 1) + arg + 1, pool_passed)
                        scatter(1 - par, arg, scattered[arg])
                    elif name == "gather":
                        if arg <= NT:
                            copy_order(b + 1, 1 - par, arg)
                        gather(b + 1, 1 - par, arg)
                    elif name == "add_w":
                        add_w(b, par, arg)
                    elif name == "scatter_tail":
                        scatter_tail(b, par, arg)

                def add_tile(s, h, k):
                    acc, p0 = t["Pacc"][:R, h % f.NA], (NT * h + k) % f.NP
                    if k == 1:
                        at_least(pool, l_ready, s - f.NA + 1)
                        other = t["Pt"][:R, (NT * h) % f.NP]
                    else:
                        pool.wait_ge(pacc_step, (NT - 1) * s + k - 1)
                        other = acc
                    pool.wait_ge(exp_done, 2 * (NT * s + k) + 2)
                    nc.gpsimd.tensor_tensor(acc, other, t["Pt"][:R, p0], ALU.add).then_inc(pacc_step, 1)

                pool.wait_ge(idx_made, 1)
                for k in range(NTALL):
                    if k <= NT:
                        copy_order(0, 0, k)
                    gather(0, 0, k)
                if f.split:
                    for i, (w, name) in enumerate(((wqT_sb, "wqT"), (woT_sb, "woT"))):
                        pool.wait_ge(whi_done, i + 1)
                        nc.gpsimd.tensor_tensor(t[name + "_lo"][:], w[:], t[name + "_hi"][:].bitcast(F32),
                                                ALU.subtract).then_inc(wlo_done, 1)
                pool.wait_ge(idx_made, 2)
                if f.split:
                    pool.wait_ge(wlo_done, 2)
                nc.gpsimd.memset(t["ops"][DK:P, :, OPX, :].bitcast(F32), 0.0).then_inc(ops_cleared, 1)
                nc.gpsimd.memset(t["ops"][DK:P, :, OPY, :].bitcast(F32), 0.0).then_inc(ops_cleared, 1)
                pool.wait_ge(ops_cleared, 2)
                nc.gpsimd.memset(t["ops"][DK:DK + 1, :, OPY, :].bitcast(F32), 1.0).then_inc(ops_cleared, 1)

                def batch(b, par, table, has_prev, has_next):
                    jobs = pool_jobs(f, has_prev, has_next)
                    for h in range(HEADS):
                        for k in range(NT):
                            if k > 0:
                                add_tile(HEADS * b + h, h, k)
                            for name, arg in jobs[h, k]:
                                job(name, arg, b, par)

                def tail(jobs):
                    for i in range(NT):
                        pool.wait_ge(out_done, NT * (B - 1) + i + 1)
                        scatter((B - 1) % 2, i, scattered[i])
                    for i in range(NT):
                        pool.wait_ge(scattered[i], 16 * B)
                    for par in range(2):
                        at_least(pool, scattered_tail[par], 8 * NTAIL * B)

                run_batches(pool, f, plan, batch, tail)

            fitting_form(pool, body)

        @block.scalar
        def _(act):
            act.wait_ge(consts_made, 8)
            def body(f, t, plan):
                NT, R, C, H = f.NT, f.R, f.C, f.H

                if f.split:
                    act.wait_ge(loaded, 48)
                    nc.scalar.copy(t["wqT_hi"][:], wqT_sb[:]).then_inc(whi_done, 1)
                    nc.scalar.copy(t["woT_hi"][:], woT_sb[:]).then_inc(whi_done, 1)
                for k in range(KD):
                    act.wait_ge(g_made, k + 1)
                    nc.scalar.copy(G[:, k, :], MB[k % 2][:, 0:D]).then_inc(g_kept, 1)

                def job(name, arg, bank, b, par):
                    if name == "xT":
                        act.wait_ge(xT_ready, NT * (b + 1) + arg + 1)
                        at_least(act, proj_ready, 2 * PAIRS * (b + 1))
                        nc.scalar.copy(t["xcT"][:, :, R * arg:R * arg + R],
                                       MB[bank][:, 0:KD * R].rearrange("p (c r) -> p c r", c=KD)).then_inc(xT_kept, 1)
                        if arg + 1 < NT:
                            zero_masked(b + 1, 1 - par, arg + 1)
                    elif name == "xbar":
                        act.wait_ge(xbar_ready, b + 2)
                        at_least(act, w_ready, b + 1)
                        nc.scalar.copy(t["xbarT"][:].rearrange("p k n -> p (k n)"), MB[bank][:, 0:KD * P]).then_inc(xbar_kept, 1)
                    elif name == "w":
                        act.wait_ge(w_ready, b + 2)
                        at_least(act, out_done, NT * b)
                        at_least(act, tail_added, f.NTAIL * b)
                        nc.scalar.copy(t["w"][:, 1 - par, :], MB[bank][:, 0:D]).then_inc(w_kept, 1)
                    elif name == "proj":
                        g, half = arg
                        p = PAIRS * b + g
                        act.wait_ge(proj_ready, 2 * p + half + 1)
                        at_least(act, lo_done, 2 * p - 2)
                        at_least(act, dup[(2 * g) % SLOTS], 96 * (2 * b + g // 2))
                        at_least(act, dup[(2 * g + 1) % SLOTS], 96 * (2 * b + g // 2))
                        at_least(act, v_ready, 2 * p - 2)
                        cols = slice(half * H, half * H + H)
                        q = MB[bank][:, 0:H]
                        if f.split:
                            nc.scalar.copy(t["Q"][:, g % 2, cols], q).then_inc(q_kept, 1)
                            act.wait_ge(q_kept, 2 * p + half + 1)
                            q = t["Q"][:, g % 2, cols]
                        nc.scalar.copy(t["H"][:, g % 2, cols], q).then_inc(hi_done, 1)
                    elif name == "V":
                        g, part = arg
                        p = PAIRS * b + g
                        n = min(4, NT - 4 * part)
                        act.wait_ge(v_ready, 2 * p + part + 1)
                        at_least(act, pv_done, NT * (2 * p - 2))
                        nc.scalar.copy(t["V"][:R, g % 2, 4 * part:4 * part + n, :],
                                       MB[bank][:R, 0:n * P].rearrange("r (k c) -> r k c", k=n)).then_inc(v_kept, 1)

                def keep_sums(s, bank):
                    act.wait_ge(l_ready, s + 1)
                    at_least(act, ctx_done, s)
                    nc.scalar.activation(t["rsum"][:], MB[bank][:, 0:H], ACT.Identity,
                                         bias=tiny[:, 0:1]).then_inc(rsum_done, 1)

                def max_row(h, b, s, bank):
                    act.wait_ge(mT_ready, s + 1)
                    at_least(act, mrow_put[h % 2], 16 * ((HEADS // 2) * b + h // 2))
                    nc.scalar.copy(t["mrow"][:, h % 2, :], MB[bank][:NT, 0:R]).then_inc(mrow_done, 1)

                def keep_ctx(s, h):
                    act.wait_ge(pv_done, NT * (s + 1))
                    at_least(act, ctx_done, s)
                    nc.scalar.copy(t["ctxraw"][:], CT[:, 0:H]).then_inc(ct_kept, 1)

                def ctx_high(b, pair):
                    act.wait_ge(ctx_done, HEADS * b + 2 * pair + 2)
                    at_least(act, out_ready, NT * b)
                    nc.scalar.copy(t["ctxT"][:, pair, :], t["ctx"][:, pair % 2, :]).then_inc(ctx_hi_done, 1)

                def zero_masked(b, par, k):
                    act.wait_ge(gathered[k], 16 * (b + 1))
                    if k == 0:
                        act.wait_ge(mask_step, 3 * (b + 1))
                    at_least(act, xT_ready, NT * b + k + 1 - f.NA)
                    nc.scalar.mul(t["xv"][:R, k % f.NA, :], t["xg"][:R, par, k, :],
                                  t["valid"][:R, par, k:k + 1]).then_inc(xv_done, 1)

                zero_masked(0, 0, 0)
                for name, arg, bank, before in plan[0]:
                    if name == "mT":
                        max_row(0, 0, 0, bank)
                    else:
                        job(name, arg, bank, 0 if name in ("proj", "V") else -1, 1)

                def batch(b, par, table, has_prev, has_next):
                    for h in range(HEADS):
                        s = HEADS * b + h
                        for k in range(NT):
                            if k == 1 and (h > 0 or has_prev):
                                keep_ctx(s - 1, h - 1)
                            n = NT * s + k
                            if h == 0 and k == 0:
                                act.wait_ge(mask_step, 3 * (b + 1))
                            at_least(act, pv_done, n - f.NP + 1)
                            ko, so = k - f.NP, s
                            while ko < 0:
                                ko, so = ko + NT, so - 1
                            at_least(act, pacc_step, (NT - 1) * so + max(ko, 1))
                            for half in range(2):
                                act.wait_ge(s_ready, 2 * n + half + 1)
                                nc.scalar.activation(t["Pt"][:R, (NT * h + k) % f.NP, half, :],
                                                     ST[(2 * (NT * h + k) + half) % 3][:R, 0:H], ACT.Exp,
                                                     bias=t["kbias"][:R, par, k:k + 1],
                                                     scale=SCALE).then_inc(exp_done, 1)
                            for name, arg, bank, before in table[h, k]:
                                if name == "L":
                                    keep_sums(s - 1, bank)
                                elif name == "mT":
                                    max_row(arg, b, s + 1, bank)
                                else:
                                    job(name, arg, bank, b, par)
                            if f.split and k == 1 and h % 2:
                                if h > 1:
                                    ctx_high(b, h // 2 - 1)
                                elif has_prev:
                                    ctx_high(b - 1, PAIRS - 1)
                            if has_next and (h, k) == masked_from(f):
                                zero_masked(b + 1, 1 - par, 0)

                def tail(jobs):
                    keep_ctx(HEADS * B - 1, HEADS - 1)
                    keep_sums(HEADS * B - 1, jobs[0][2])
                    if f.split:
                        ctx_high(B - 1, PAIRS - 1)

                run_batches(act, f, plan, batch, tail)

            fitting_form(act, body)

        @block.vector
        def _(dve):
            dve.wait_ge(mask_loaded, 16)
            nc.vector.tensor_copy(mask_b[:], mask_f[:]).then_inc(mask_cast, 1)
            dve.wait_ge(iotas_made, 1)
            nc.vector.tensor_copy(tokid[:], tokid_i[:]).then_inc(pos_step, 1)
            dve.wait_ge(consts_made, 8)
            nc.vector.tensor_copy(identR[:], ident[:]).then_inc(consts_cast, 1)
            dve.wait_ge(counted, 1)
            nc.vector.tensor_copy(cnt[:].rearrange("p t b -> p (t b)"), ST[0][:, 0:TT * B]).then_inc(pos_step, 1)
            nc.vector.tensor_copy(n_all[:], ST[1][:, 0:B]).then_inc(pos_step, 1)
            dve.wait_ge(pos_step, 3)
            nc.vector.tensor_tensor(behind[:], tokid[:], cnt[:], ALU.subtract).then_inc(pos_step, 1)
            nc.vector.tensor_reduce(n_max[:], n_all[:], AX.X, ALU.max).then_inc(pos_step, 1)
            dve.wait_ge(pos_step, 5)
            nc.vector.tensor_tensor(behind[:], behind[:], n_all[:].unsqueeze(1).to_broadcast([P, TT, B]),
                                    ALU.add).then_inc(pos_step, 1)
            nc.vector.tensor_copy(n_max_i[:], n_max[:]).then_inc(pos_done, 1)
            dve.wait_ge(pos_step, 6)
            nc.vector.scalar_tensor_tensor(out=cnt[:], in0=cnt[:], scalar=-1.0, in1=behind[:], op0=ALU.add,
                                           op1=ALU.subtract).then_inc(pos_step, 1)
            dve.wait_ge(pos_step, 7)
            nc.vector.tensor_tensor(cnt[:], cnt[:], mask_f[:], ALU.mult).then_inc(pos_step, 1)
            dve.wait_ge(pos_step, 8)
            nc.vector.tensor_tensor(pos[:], cnt[:], behind[:], ALU.add).then_inc(pos_done, 1)

            def body(f, t, plan):
                NT, R, C, H, NTALL = f.NT, f.R, f.C, f.H, f.NTALL
                chain = 0

                dve.wait_ge(iotas_made, 5)
                nc.vector.tensor_copy(t["tileno"][:], t["tileno_i"][:]).then_inc(place_step, 1)
                nc.vector.tensor_copy(t["rowno"][:], t["rowno_i"][:]).then_inc(place_step, 1)
                nc.vector.tensor_copy(t["jidx"][:], t["jidx_i"][:]).then_inc(jidx_made, 1)
                nc.vector.tensor_copy(t["boff"][:], t["boff_i"][:]).then_inc(place_step, 1)
                nc.vector.tensor_scalar(t["jh"][:], pos[:], float(R), None, ALU.is_ge).then_inc(place_step, 1)
                chain = 4
                for i in range(2, NTALL):
                    dve.wait_ge(place_step, chain)
                    nc.vector.scalar_tensor_tensor(out=t["jh"][:], in0=pos[:], scalar=float(R * i), in1=t["jh"][:],
                                                   op0=ALU.is_ge, op1=ALU.add).then_inc(place_step, 1)
                    chain += 1
                dve.wait_ge(place_step, chain)
                nc.vector.scalar_tensor_tensor(out=t["jl"][:], in0=t["jh"][:], scalar=-float(R), in1=pos[:],
                                               op0=ALU.mult, op1=ALU.add).then_inc(place_step, 1)
                hot_shape = [P, TT * B, NTALL]
                flat = lambda a: a[:].rearrange("p t b -> p (t b)").unsqueeze(2).to_broadcast(hot_shape)
                hot_f = t["hot_tile_f"][:].rearrange("p t b i -> p (t b) i")
                nc.vector.tensor_tensor(hot_f, t["tileno"][:].unsqueeze(1).to_broadcast(hot_shape), flat(t["jh"]),
                                        ALU.is_equal).then_inc(place_step, 1)
                chain += 2
                dve.wait_ge(place_step, chain)
                nc.vector.tensor_tensor(t["hot_tile"][:].rearrange("p t b i -> p (t b) i"), hot_f, flat(tokid),
                                        ALU.mult).then_inc(onehots_made, 1)
                nc.vector.tensor_tensor(t["hot_row"][:, :, 0], t["rowno"][:].unsqueeze(1).to_broadcast([P, TT, R]),
                                        t["jl"][:, :, 0].unsqueeze(2).to_broadcast([P, TT, R]),
                                        ALU.is_equal).then_inc(onehots_made, 1)
                for tt in range(TT):
                    nc.vector.tensor_tensor(t["hot_row"][:, tt, 1:], t["rowno"][:].unsqueeze(1).to_broadcast([P, B - 1, R]),
                                            t["jl"][:, tt, 1:].unsqueeze(2).to_broadcast([P, B - 1, R]),
                                            ALU.is_equal).then_inc(onehots_made, 1)
                    if tt == 0:
                        dve.wait_ge(perm_made, 1)
                        nc.vector.tensor_tensor(t["idx"][:R, 0], ST[0][:R, 0:NTALL], t["boff"][:R, 0],
                                                ALU.add).then_inc(idx_made, 1)

                def masks(b, par):
                    n = n_all[:, bass.ds(b, 1)]
                    j = t["jidx"][:, 0:NT]
                    at_least(dve, exp_done, 2 * NT * HEADS * (b - 1))
                    at_least(dve, out_done, NT * (b - 1))
                    nc.vector.tensor_scalar(t["valid"][:, par, :], j, n, None, ALU.is_lt).then_inc(mask_step, 1)
                    nc.vector.tensor_scalar(t["inv"][:, par, :], j, n, None, ALU.is_ge).then_inc(mask_step, 1)
                    nc.vector.tensor_scalar(t["kbias"][:, par, :], j, n, NEG, ALU.is_ge, ALU.mult).then_inc(mask_step, 1)
                    dve.wait_ge(mask_step, 3 * (b + 1))

                def sum_tokens(b, par, k):
                    acc, r = t["xsum"], f.rows(k)
                    if k == 1:
                        for i in range(NT):
                            dve.wait_ge(gathered[i], 16 * (b + 1))
                        at_least(dve, xbar_ready, b)
                        other = t["xg"][:R, par, 0, :]
                    else:
                        dve.wait_ge(xsum_step, (NTALL - 1) * b + k - 1)
                        other = acc[:r]
                    if k == NT:
                        at_least(dve, gathered_tail, 16 * f.NTAIL * (b + 1))
                    nc.vector.tensor_tensor(acc[:r], other, t["xg"][:r, par, k, :], ALU.add).then_inc(xsum_step, 1)

                def reduce_max(s, h, m):
                    dve.wait_ge(mx_ready, 2 * NT * s + m + 1)
                    nc.vector.tensor_reduce(t["mxp"][:R, h % 2, m // 2, m % 2:m % 2 + 1], MX[m % 2][:R, 0:H], AX.X,
                                            ALU.max).then_inc(mx_red, 1)
                    if m == 2 * NT - 1:
                        dve.wait_ge(mx_red, 2 * NT * (s + 1))
                        at_least(dve, mT_ready, s - 1)
                        nc.vector.tensor_reduce(t["mcol"][:R, h % 2, :], t["mxp"][:R, h % 2], AX.X, ALU.max,
                                                negate=True).then_inc(mcol_done, 1)

                def job(name, arg, bank, b, par, s):
                    if name == "proj":
                        g, half = arg
                        p = PAIRS * b + g
                        dve.wait_ge(hi_done, 2 * p + half + 1)
                        cols = slice(half * H, half * H + H)
                        q = t["Q"][:, g % 2, cols] if f.split else MB[bank][:, 0:H]
                        nc.vector.tensor_tensor(t["L"][:, g % 2, cols], q,
                                                t["H"][:, g % 2, cols].bitcast(F32), ALU.subtract).then_inc(lo_done, 1)
                    elif name == "out":
                        finish_tile(b - 1, 1 - par, arg, bank)
                    elif name == "xT" and f.split:
                        dve.wait_ge(xT_kept, NT * (b + 1) + arg + 1)
                        cols = slice(R * arg, R * arg + R)
                        nc.vector.tensor_tensor(t["xcT_lo"][:, :, cols],
                                                MB[bank][:, 0:KD * R].rearrange("p (c r) -> p c r", c=KD),
                                                t["xcT"][:, :, cols].bitcast(F32), ALU.subtract).then_inc(xlo_done, 1)

                def reciprocal(s, quarter):
                    dve.wait_ge(rsum_done, s + 1)
                    cols = slice(H * quarter // 4, H * (quarter + 1) // 4)
                    nc.vector.reciprocal(t["rsum"][:, cols], t["rsum"][:, cols]).then_inc(recip_step, 1)

                def ctx_low(b, pair):
                    dve.wait_ge(ctx_hi_done, PAIRS * b + pair + 1)
                    nc.vector.tensor_tensor(t["ctxT_lo"][:, pair, :], t["ctx"][:, pair % 2, :],
                                            t["ctxT"][:, pair, :].bitcast(F32), ALU.subtract).then_inc(ctx_lo_done, 1)

                def scale(s, h, b, par, half):
                    if half == 0:
                        dve.wait_ge(recip_step, 4 * (s + 1))
                        dve.wait_ge(ct_kept, s + 1)
                        if f.split:
                            at_least(dve, ctx_lo_done, PAIRS * b + h // 2 - 1)
                        elif h == 0:
                            at_least(dve, out_ready, NT * b)
                    r0, pr, cols = DK * half, DK * (h % 2), slice(half * H, half * H + H)
                    last = nc.vector.tensor_tensor(
                        t["ctx"][pr:pr + DK, h // 2 % 2, cols] if f.split else t["ctxT"][pr:pr + DK, h // 2, cols],
                        t["rsum"][r0:r0 + DK, :], t["ctxraw"][r0:r0 + DK, :], ALU.mult)
                    if half == 1:
                        last.then_inc(ctx_done, 1)

                def alone(name, arg, b, par, h):
                    if name == "reciprocal":
                        reciprocal(HEADS * b + h, arg)
                    elif name == "scale":
                        if h < 0:
                            scale(HEADS * b + h, HEADS + h, b - 1, 1 - par, arg)
                        else:
                            scale(HEADS * b + h, h, b, par, arg)
                    elif name == "ctx_low":
                        if h < 0:
                            ctx_low(b - 1, PAIRS - 1)
                        else:
                            ctx_low(b, h // 2)
                    elif name == "masks":
                        masks(b + 1, 1 - par)
                    elif name == "sum_tokens":
                        sum_tokens(b + 1, 1 - par, arg)

                def finish_tile(b, par, k, bank):
                    xk = t["xg"][:R, par, k, :]
                    dve.wait_ge(out_ready, NT * b + k + 1)
                    dve.wait_ge(w_kept, b + 1)
                    at_least(dve, out_done, NT * b + k)
                    nc.vector.scalar_tensor_tensor(out=t["xsum"][:R], in0=MB[bank][:R, 0:D],
                                                   scalar=t["valid"][:R, par, k:k + 1], in1=xk, op0=ALU.mult,
                                                   op1=ALU.add).then_inc(out_step, 1)
                    dve.wait_ge(out_step, NT * b + k + 1)
                    nc.vector.scalar_tensor_tensor(out=xk, in0=t["w"][:R, par, :], scalar=t["inv"][:R, par, k:k + 1],
                                                   in1=t["xsum"][:R], op0=ALU.mult, op1=ALU.add).then_inc(out_done, 1)

                masks(0, 0)
                dve.wait_ge(perm_made, B)
                nc.vector.tensor_tensor(t["idx"][:R, 1:],
                                        ST[2][:R, NTALL:B * NTALL].rearrange("p (b i) -> p b i", b=B - 1),
                                        t["boff"][:R, 1:], ALU.add).then_inc(idx_made, 1)
                quarter = -(-(NTALL - 1) // 4)
                for name, arg, bank, before in plan[0]:
                    if name == "mT":
                        for m in range(2 * NT):
                            reduce_max(0, 0, m)
                    job(name, arg, bank, -1 if name == "xT" else 0, 1 if name == "xT" else 0, 0)
                    if name == "mT":
                        for m in range(2 * NT):
                            reduce_max(1, 1, m)
                    if name == "proj" and arg[0] < 2:
                        first = 1 + (2 * arg[0] + arg[1]) * quarter
                        for k in range(first, min(first + quarter, NTALL)):
                            sum_tokens(0, 0, k)

                def batch(b, par, table, has_prev, has_next):
                    extras = vector_jobs(f, has_prev, has_next)
                    late = []
                    for h in range(HEADS):
                        s = HEADS * b + h
                        for k in range(NT):
                            for a in range(2):
                                if h < HEADS - 2 or has_next:
                                    reduce_max(s + 2, h + 2, 2 * k + a)
                                due = [j for j in table[h, k] if j[0] not in LATE] if a == 1 else late
                                for name, arg, bank, before in due:
                                    job(name, arg, bank, b, par, s + 1 if name == "mT" else s - 1)
                                if a == 1:
                                    late = [j for j in table[h, k] if j[0] in LATE]
                                for name, arg in extras[h, k, a]:
                                    alone(name, arg, b, par, h - 1 if k > 0 and name != "ctx_low" else h - 2)
                    assert not late

                def tail(jobs):
                    if f.split:
                        alone("scale", 1, B, B % 2, -2)
                    for name, arg, bank, before in jobs:
                        job(name, arg, bank, B, B % 2, HEADS * B - 1)
                        if name == "L":
                            for quarter in range(4):
                                alone("reciprocal", quarter, B, B % 2, -1)
                            for half in range(2):
                                alone("scale", half, B, B % 2, -1)
                            if f.split:
                                alone("ctx_low", 0, B, B % 2, -1)

                run_batches(dve, f, plan, batch, tail)

            fitting_form(dve, body)

        @block.tensor
        def _(pe):
            pe.wait_ge(consts_made, 8)
            pe.wait_ge(mask_cast, 1)
            for tt in range(TT):
                for u in range(tt + 1):
                    nc.tensor.matmul(ST[0][:, B * tt:B * tt + B], tri[:] if u == tt else ones_b[:], mask_b[:, u, :],
                                     start=(u == 0), stop=(u == tt))
            for u in range(TT):
                last = nc.tensor.matmul(ST[1][:, 0:B], ones_b[:], mask_b[:, u, :], start=(u == 0), stop=(u == TT - 1))
            last.then_inc(counted, 1)

            def body(f, t, plan):
                NT, R, C, H, NTALL = f.NT, f.R, f.C, f.H, f.NTALL

                def order(b, bank, col):
                    for tt in range(TT):
                        last = nc.tensor.matmul(bank[:R, col], t["hot_row"][:, tt, b, :], t["hot_tile"][:, tt, b, :],
                                                start=(tt == 0), stop=(tt == TT - 1))
                    last.then_inc(perm_made, 1)

                pe.wait_ge(onehots_made, 2)
                order(0, ST[0], slice(0, NTALL))
                pe.wait_ge(loaded, 48)
                for k in range(KD):
                    at_least(pe, g_kept, k - 1)
                    for m in range(KD):
                        last = nc.tensor.matmul(MB[k % 2][:, 0:D], wq_sb[:, m, P * k:P * k + P], woT_sb[:, m, :],
                                                start=(m == 0), stop=(m == KD - 1))
                    last.then_inc(g_made, 1)

                pe.wait_ge(onehots_made, TT + 2)
                group = next(n for n in (5, 3, 2, 1) if (B - 1) % n == 0)
                with pe.Fori(0, (B - 1) // group) as g:
                    for i in range(1, group + 1):
                        order(g * group + i, ST[2], bass.ds((g * group + i) * NTALL, NTALL))
                pe.wait_ge(g_kept, KD)

                def tile_cols(i):
                    return slice(R * i, R * i + R)

                def half_cols(i):
                    return slice(H * i, H * i + H)

                def pair_cols(i):
                    return slice(P * i, P * i + P)

                def max_scores(s, s4, h, m):
                    ops = t["ops"][:, h % SLOTS]
                    if m == 0:
                        pe.wait_ge(dup[h % SLOTS], 96 * (s4 + 1))
                    at_least(pe, mx_red, 2 * NT * s + m - 1)
                    nc.tensor.matmul(MX[m % 2][:R, 0:H], ops[:, OPA, tile_cols(m // 2)], ops[:, OPB, half_cols(m % 2)],
                                     start=True, stop=True).then_inc(mx_ready, 1)

                def scores(s, s2, h, k):
                    ops = t["ops"][:, h % SLOTS]
                    if k == 0:
                        pe.wait_ge(mrow_put[h % 2], 16 * (s2 + 1))
                    banks, count = [], 2 * NT * HEADS
                    for half in range(2):
                        u = 2 * (NT * h + k) + half
                        banks.append(ST[u % 3])
                        last_user = u - 3 if u >= 3 else next(v for v in range(-1, -4, -1) if (count + v - u) % 3 == 0)
                        at_least(pe, exp_done, 2 * NT * (s - h) + last_user + 1)
                        nc.tensor.matmul(banks[half][:R, 0:H], ops[:, OPA, tile_cols(k)], ops[:, OPB, half_cols(half)],
                                         start=True, stop=False)
                    for half in range(2):
                        nc.tensor.matmul(banks[half][:R, 0:H], ops[:, OPY, tile_cols(k)], ops[:, OPX, half_cols(half)],
                                         start=False, stop=True).then_inc(s_ready, 1)

                def times_values(s, p, h, k):
                    if k == 0:
                        at_least(pe, ct_kept, s)
                        at_least(pe, v_kept, 2 * p + 2)
                    for half in range(2):
                        pe.wait_ge(exp_done, 2 * (NT * s + k) + half + 1)
                        last = nc.tensor.matmul(CT[DK * half:DK * half + DK, 0:H],
                                                t["V"][:R, (h // 2) % 2, k, DK * (h % 2):DK * (h % 2) + DK],
                                                t["Pt"][:R, (NT * h + k) % f.NP, half, :],
                                                start=(k == 0), stop=(k == NT - 1))
                    last.then_inc(pv_done, 1)

                def bank_left(name, arg, b):
                    if name == "xT":
                        at_least(pe, xlo_done if f.split else xT_kept, NT * (b + 1) + arg + 1)
                    elif name == "xbar":
                        at_least(pe, xbar_kept, b + 2)
                    elif name == "w":
                        at_least(pe, w_kept, b + 2)
                    elif name == "proj":
                        at_least(pe, q_kept if f.split else lo_done, 2 * (PAIRS * b + arg[0]) + arg[1] + 1)
                    elif name == "V":
                        at_least(pe, v_kept, 2 * (PAIRS * b + arg[0]) + arg[1] + 1)
                    elif name == "mT":
                        at_least(pe, mrow_done, HEADS * b + arg + 1)
                    elif name == "L":
                        at_least(pe, rsum_done, HEADS * b + arg + 1)
                    elif name == "out":
                        at_least(pe, out_step, NT * (b - 1) + arg + 1)

                def product(out, left, left_whole, left_at, right, right_whole, right_at, c):
                    if not f.split:
                        return nc.tensor.matmul(out, left_whole[left_at], right_whole[right_at],
                                                start=(c == 0), stop=(c == KD - 1))
                    lefts = [t[n] for n in ((left + "_hi", left + "_lo") if left == "wqT" else (left, left + "_lo"))]
                    rights = [t[n] for n in ((right + "_hi", right + "_lo") if right == "woT" else (right, right + "_lo"))]
                    for i, (a, z) in enumerate(((0, 0), (0, 1), (1, 0))):
                        last = nc.tensor.matmul(out, lefts[a][left_at], rights[z][right_at],
                                                start=(c == 0 and i == 0), stop=(c == KD - 1 and i == 2))
                    return last

                def job(name, arg, bank, before, b, par, s, chunks=range(KD)):
                    mb = MB[bank]
                    if before and chunks[0] == 0:
                        bank_left(before[0], before[1], b + before[2])
                    if name == "xT":
                        pe.wait_ge(xv_done, NT * (b + 1) + arg + 1)
                        for c in range(KD):
                            last = nc.tensor.transpose(mb[:, R * c:R * c + R], t["xv"][:R, arg % f.NA, P * c:P * c + P],
                                                       ident[:R, :R])
                        last.then_inc(xT_ready, 1)
                    elif name == "xbar":
                        pe.wait_ge(xsum_step, (NTALL - 1) * (b + 2))
                        for c in range(KD):
                            last = nc.tensor.matmul(mb[:, P * c:P * c + P], t["xsum"][:R, P * c:P * c + P], meanT[:R, :],
                                                    start=True, stop=True)
                        last.then_inc(xbar_ready, 1)
                    elif name == "w":
                        if chunks[0] == 0:
                            pe.wait_ge(xbar_kept, b + 2)
                        for c in chunks:
                            last = nc.tensor.matmul(mb[:, 0:D], t["xbarT"][:, c, :], G[:, c, :],
                                                    start=(c == 0), stop=(c == KD - 1))
                        if c == KD - 1:
                            last.then_inc(w_ready, 1)
                    elif name == "proj":
                        g, half = arg
                        if chunks[0] == 0:
                            pe.wait_ge(xlo_done if f.split else xT_kept, NT * (b + g // PAIRS + 1))
                        for c in chunks:
                            last = product(mb[:, 0:H], "wqT", wqT_sb, (slice(None), c, pair_cols(g % PAIRS)),
                                           "xcT", t["xcT"], (slice(None), c, half_cols(half)), c)
                        if c == KD - 1:
                            last.then_inc(proj_ready, 1)
                    elif name == "V":
                        g, part = arg
                        pe.wait_ge(q_kept if f.split else lo_done, 2 * (PAIRS * b + g) + 2)
                        for i in range(min(4, NT - 4 * part)):
                            cols = tile_cols(4 * part + i)
                            if f.split:
                                last = nc.tensor.transpose(mb[:R, P * i:P * i + P], t["Q"][:, g % 2, cols], ident[:])
                                continue
                            nc.tensor.matmul(mb[:R, P * i:P * i + P], t["H"][:, g % 2, cols], identR[:],
                                             start=True, stop=False)
                            last = nc.tensor.matmul(mb[:R, P * i:P * i + P], t["L"][:, g % 2, cols], identR[:],
                                                    start=False, stop=True)
                        last.then_inc(v_ready, 1)
                    elif name == "mT":
                        pe.wait_ge(mcol_done, s + 1)
                        nc.tensor.transpose(mb[:NT, 0:R], t["mcol"][:R, arg % 2, :], ident[:R, :R]).then_inc(mT_ready, 1)
                    elif name == "L":
                        pe.wait_ge(pacc_step, (NT - 1) * (s + 1))
                        for half in range(2):
                            last = nc.tensor.matmul(mb[DK * half:DK * half + DK, 0:H], ones64[:R, :],
                                                    t["Pacc"][:R, arg % HEADS % f.NA, half, :], start=True, stop=True)
                        last.then_inc(l_ready, 1)
                    elif name == "out":
                        if chunks[0] == 0:
                            pe.wait_ge(ctx_lo_done if f.split else ctx_done, (PAIRS if f.split else HEADS) * b)
                        for c in chunks:
                            last = product(mb[:R, 0:D], "ctxT", t["ctxT"],
                                           (slice(None), c, tile_cols(arg)),
                                           "woT", woT_sb, (slice(None), c, slice(None)), c)
                        if c == KD - 1:
                            last.then_inc(out_ready, 1)

                if f.split:
                    pe.wait_ge(wlo_done, 2)
                for (name, arg, bank, before), (_, _, b) in zip(plan[0], front_jobs(f)):
                    if before:
                        bank_left(*before)
                    if name == "mT":
                        for m in range(2 * NT):
                            max_scores(0, 0, 0, m)
                    if name == "xbar":
                        for m in range(2 * NT):
                            max_scores(1, 0, 1, m)
                    job(name, arg, bank, None, b, b % 2, 0)

                def misc(jobs, b, par, s, part):
                    for name, arg, bank, before in jobs:
                        sj = s + 1 if name == "mT" else s - 1
                        if name in TWO_PARTS:
                            job(name, arg, bank, before, b, par, sj, range(KD // 2 * part, KD // 2 * (part + 1)))
                        elif part == (name in ("xT", "mT")):
                            job(name, arg, bank, before, b, par, sj)

                def batch(b, par, table, has_prev, has_next):
                    for h in range(HEADS):
                        s = HEADS * b + h
                        for k in range(NT):
                            ahead = h < HEADS - 2 or has_next
                            if ahead:
                                max_scores(s + 2, 2 * b + (h + 2) // SLOTS, h + 2, 2 * k)
                            scores(s, (HEADS // 2) * b + h // 2, h, k)
                            misc(table[h, k], b, par, s, 0)
                            if ahead:
                                max_scores(s + 2, 2 * b + (h + 2) // SLOTS, h + 2, 2 * k + 1)
                            if k > 0:
                                times_values(s, PAIRS * b + h // 2, h, k - 1)
                            elif h > 0:
                                times_values(s - 1, PAIRS * b + (h - 1) // 2, h - 1, NT - 1)
                            elif has_prev:
                                times_values(s - 1, PAIRS * b - 1, HEADS - 1, NT - 1)
                            misc(table[h, k], b, par, s, 1)

                def tail(jobs):
                    times_values(HEADS * B - 1, PAIRS * B - 1, HEADS - 1, NT - 1)
                    for name, arg, bank, before in jobs:
                        job(name, arg, bank, before, B, B % 2, HEADS * B - 1)

                run_batches(pe, f, plan, batch, tail)

            fitting_form(pe, body)


def kernel(x, cond_2048, L0_cond_Wq, L0_cond_Wo):
    import numpy as np
    import concourse.bacc as bacc
    from concourse.bass_utils import run_bass_kernel_spmd

    x = np.asarray(x)
    B, D, T = x.shape
    mask = np.asarray(cond_2048)
    wq, wo = np.asarray(L0_cond_Wq), np.asarray(L0_cond_Wo)
    arrays = {
        "x_rows": np.ascontiguousarray(x.transpose(0, 2, 1)).reshape(B * T, D),
        "mask_t": np.ascontiguousarray(mask.reshape(B, T // P, P).transpose(2, 1, 0)).reshape(P, -1),
        "wq": np.ascontiguousarray(wq),
        "wqT": np.ascontiguousarray(wq.T),
        "woT": np.ascontiguousarray(wo.T),
    }
    nc = bacc.Bacc("TRN2", target_bir_lowering=False, num_devices=1)
    ins = [nc.dram_tensor(n, a.shape, F32, kind="ExternalInput").ap() for n, a in arrays.items()]
    out = nc.dram_tensor("out_rows", (B * T, D), F32, kind="ExternalOutput").ap()
    attention_kernel(nc, *ins, out, B, T, D)
    got = run_bass_kernel_spmd(nc, [arrays], core_ids=[0]).results[0]["out_rows"]
    return np.ascontiguousarray(got.reshape(B, T, D).transpose(0, 2, 1))
```
